# Optimizing a Trainium2 kernel written in Bass

```python
import numpy as np
import jax
import jax.numpy as jnp

def _softmax(x, axis=-1):
    return jax.nn.softmax(x, axis=axis)

def _gelu(x):
    return jax.nn.gelu(x, approximate=True)

def _silu(x):
    return jax.nn.silu(x)

def _sigmoid(x):
    return jax.nn.sigmoid(x)

def _layernorm(x, axis=-1, eps=1e-05):
    m = jnp.mean(x, axis=axis, keepdims=True)
    v = jnp.var(x, axis=axis, keepdims=True)
    return (x - m) / jnp.sqrt(v + eps)

def _scatter_add(tgt, idx, src, axis=0):
    return tgt.at[idx].add(src)

def _segment_sum(src, seg, n):
    return jax.ops.segment_sum(src, seg, n)
kernel_name = 'mk_adj_preln_d4_adj_r2_f394b6'

def setup_inputs(seed: int=0):
    np.random.seed(seed)
    _w = jnp.asarray

    def _rec_inputs():
        import jax
        import jax.numpy as jnp
        _gk = jax.random.key(seed)
        x = -0.0002928 + 1 * jax.random.normal(jax.random.fold_in(_gk, 1), (32, 256, 128), jnp.float32)
        _a = jax.random.bernoulli(jax.random.fold_in(_gk, 2), 0.0078125, (32, 256, 256))
        _a = jnp.logical_or(_a, jnp.swapaxes(_a, -1, -2))
        _a = jnp.logical_or(_a, jnp.eye(256, dtype=bool))
        adj = _a.astype(jnp.int32)
        return (x, adj)
    x, adj = _rec_inputs()

    def _L0_gnn_setup():
        import jax, jax.numpy as jnp
        import numpy as np
        key = jax.random.key(seed)
        k1, k2, k3, k4 = jax.random.split(key, 4)
        B, N, F, U = (8, 2048, 128, 128)
        x = jax.random.normal(k1, (B, N, F), dtype=jnp.float32)
        adj = jax.random.randint(k2, (B, N, N), 0, 2, dtype=jnp.int32)
        W_msg = jax.random.normal(k3, (F, U), dtype=jnp.float32) * 0.05
        W_upd = jax.random.normal(k4, (F, U), dtype=jnp.float32) * 0.05
        bias = jnp.zeros((U,), dtype=jnp.float32)
        return {'x': x, 'adj': adj, 'W_msg': W_msg, 'W_upd': W_upd, 'bias': bias}
    _L0_gnn_all = _L0_gnn_setup()
    _L0_gnn_in = {k: v for k, v in _L0_gnn_all.items() if k in ('W_msg', 'W_upd', 'bias')}
    del _L0_gnn_all

    def _L1_gnn_setup():
        import jax, jax.numpy as jnp
        import numpy as np
        B, N, DIN, H, D = (16, 512, 128, 4, 32)
        NEG = -9000000000000000.0
        key = jax.random.key(seed)
        k1, k2, k3, k4 = jax.random.split(key, 4)
        x = jax.random.normal(k1, (B, N, DIN), jnp.float32)
        adj = jax.random.randint(k2, (B, N, N), 0, 2, jnp.int32)
        W = jax.random.normal(k3, (DIN, H * D), jnp.float32) * np.float32(1.0 / np.sqrt(DIN))
        b = jnp.zeros((H * D,), jnp.float32)
        a = jax.random.normal(k4, (2 * D, 1), jnp.float32) * np.float32(0.1)
        return {'x': x, 'adj': adj, 'W': W, 'b': b, 'a': a}
    _L1_gnn_all = _L1_gnn_setup()
    _L1_gnn_in = {k: v for k, v in _L1_gnn_all.items() if k in ('W', 'b', 'a')}
    del _L1_gnn_all

    def _L2_gnn_setup():
        import jax, jax.numpy as jnp
        import numpy as np
        EPS = 1e-05
        NEG = jnp.float32(-9000000000000000.0)

        def _leaky(z):
            return jnp.where(z >= 0, z, 0.01 * z)
        key = jax.random.key(seed)
        ks = jax.random.split(key, 12)
        B, N, d_in, d_hid, d_out = (4, 256, 128, 128, 128)
        d_mid = d_in // 2
        s = lambda fan: 1.0 / np.sqrt(fan)
        inp = {'x': jax.random.normal(ks[0], (B, N, d_in), dtype=jnp.float32), 'A_init': jax.random.randint(ks[1], (B, N, N), 0, 2, dtype=jnp.int32), 'W1': jax.random.normal(ks[2], (d_mid, d_in), dtype=jnp.float32) * s(d_in), 'b1': jnp.zeros((d_mid,), dtype=jnp.float32), 'g1': jnp.ones((d_mid,), dtype=jnp.float32), 'be1': jnp.zeros((d_mid,), dtype=jnp.float32), 'W2': jax.random.normal(ks[3], (1, d_mid), dtype=jnp.float32) * s(d_mid), 'b2': jnp.zeros((1,), dtype=jnp.float32), 'Wg': jax.random.normal(ks[4], (d_hid, d_in), dtype=jnp.float32) * s(d_in), 'bg': jnp.zeros((d_hid,), dtype=jnp.float32), 'gg': jnp.ones((d_hid,), dtype=jnp.float32), 'beg': jnp.zeros((d_hid,), dtype=jnp.float32), 'Wt': jax.random.normal(ks[5], (d_out, d_in + d_hid), dtype=jnp.float32) * s(d_in + d_hid), 'bt': jnp.zeros((d_out,), dtype=jnp.float32)}
        return inp
    _L2_gnn_all = _L2_gnn_setup()
    _L2_gnn_in = {k: v for k, v in _L2_gnn_all.items() if k in ('W1', 'b1', 'g1', 'be1', 'W2', 'b2', 'Wg', 'bg', 'gg', 'beg', 'Wt', 'bt')}
    del _L2_gnn_all

    def _L3_gnn_setup():
        import jax, jax.numpy as jnp
        import numpy as np
        import math
        INPUT_SIZE = 128
        key = jax.random.key(seed)
        k1, k2 = jax.random.split(key)
        B, N, D = (4, 2048, INPUT_SIZE)
        inp = jax.random.normal(k1, (B, N, D), dtype=jnp.float32)
        adj = jax.random.randint(k2, (B, N, N), 0, 2, dtype=jnp.int32)
        return {'input': inp, 'adj': adj}
    _L3_gnn_all = _L3_gnn_setup()
    _L3_gnn_in = {k: v for k, v in _L3_gnn_all.items() if k in ()}
    del _L3_gnn_all
    return {'x': x, 'adj': adj, 'L0_gnn_W_msg': _L0_gnn_in['W_msg'], 'L0_gnn_W_upd': _L0_gnn_in['W_upd'], 'L0_gnn_bias': _L0_gnn_in['bias'], 'L1_gnn_W': _L1_gnn_in['W'], 'L1_gnn_b': _L1_gnn_in['b'], 'L1_gnn_a': _L1_gnn_in['a'], 'L2_gnn_W1': _L2_gnn_in['W1'], 'L2_gnn_b1': _L2_gnn_in['b1'], 'L2_gnn_g1': _L2_gnn_in['g1'], 'L2_gnn_be1': _L2_gnn_in['be1'], 'L2_gnn_W2': _L2_gnn_in['W2'], 'L2_gnn_b2': _L2_gnn_in['b2'], 'L2_gnn_Wg': _L2_gnn_in['Wg'], 'L2_gnn_bg': _L2_gnn_in['bg'], 'L2_gnn_gg': _L2_gnn_in['gg'], 'L2_gnn_beg': _L2_gnn_in['beg'], 'L2_gnn_Wt': _L2_gnn_in['Wt'], 'L2_gnn_bt': _L2_gnn_in['bt']}

def reference(x, adj, L0_gnn_W_msg, L0_gnn_W_upd, L0_gnn_bias, L1_gnn_W, L1_gnn_b, L1_gnn_a, L2_gnn_W1, L2_gnn_b1, L2_gnn_g1, L2_gnn_be1, L2_gnn_W2, L2_gnn_b2, L2_gnn_Wg, L2_gnn_bg, L2_gnn_gg, L2_gnn_beg, L2_gnn_Wt, L2_gnn_bt):
    import jax
    import jax.numpy as jnp

    def _L0_gnn_ref(x, adj, W_msg, W_upd, bias):
        import jax, jax.numpy as jnp
        import numpy as np
        a = (adj != 0).astype(x.dtype)
        deg = jnp.sum(a, axis=1)
        msum = jnp.einsum('bij,bif->bjf', a, x)
        mean = msum / jnp.maximum(deg, 1.0)[..., None]
        messages = jnp.einsum('bnf,fu->bnu', mean, W_msg)
        xu = jnp.einsum('bnf,fu->bnu', x, W_upd)
        out = xu + messages + bias
        return jax.nn.relu(out)

    def _L1_gnn_ref(x, adj, W, b, a):
        import jax, jax.numpy as jnp
        import numpy as np
        B, N, DIN, H, D = (16, 512, 128, 4, 32)
        NEG = -9000000000000000.0
        Bb, Nn, _ = x.shape
        h = (x @ W + b).reshape(Bb, Nn, H, D)
        a_i, a_j = (a[:D, 0], a[D:, 0])
        e_i = jnp.einsum('bnhd,d->bnh', h, a_i)
        e_j = jnp.einsum('bnhd,d->bnh', h, a_j)
        e = e_i[:, :, None, :] + e_j[:, None, :, :]
        e = jnp.where(e > 0, e, 0.2 * e)
        e = jnp.where(adj[..., None] > 0, e, NEG)
        attn = jax.nn.softmax(e, axis=2)
        out = jnp.einsum('bijh,bjhd->bihd', attn, h)
        return out.reshape(Bb, Nn, H * D)

    def _L2_gnn_ref(x, A_init, W1, b1, g1, be1, W2, b2, Wg, bg, gg, beg, Wt, bt):
        import jax, jax.numpy as jnp
        import numpy as np
        EPS = 1e-05
        NEG = jnp.float32(-9000000000000000.0)

        def _leaky(z):
            return jnp.where(z >= 0, z, 0.01 * z)
        D = jnp.abs(x[:, :, None, :] - x[:, None, :, :])
        h = jnp.einsum('bijc,oc->bijo', D, W1) + b1
        m = jnp.mean(h, axis=(0, 1, 2))
        v = jnp.mean((h - m) ** 2, axis=(0, 1, 2))
        h = (h - m) / jnp.sqrt(v + EPS) * g1 + be1
        h = _leaky(h)
        s = jnp.einsum('bijo,uo->biju', h, W2)[..., 0] + b2[0]
        s = jnp.where(A_init > 0, s, NEG)
        A = jax.nn.softmax(s, axis=-1)
        y = jnp.einsum('bij,bjc->bic', A, x)
        y = y @ Wg.T + bg
        mg = jnp.mean(y, axis=(0, 1))
        vg = jnp.mean((y - mg) ** 2, axis=(0, 1))
        y = (y - mg) / jnp.sqrt(vg + EPS) * gg + beg
        y = _leaky(y)
        out = jnp.concatenate([x, y], axis=2) @ Wt.T + bt
        return out

    def _L3_gnn_ref(input, adj):
        import jax, jax.numpy as jnp
        import numpy as np
        import math
        INPUT_SIZE = 128
        scores = jnp.matmul(input, jnp.swapaxes(input, 1, 2)) / math.sqrt(INPUT_SIZE)
        neg = jnp.asarray(-1000000000000.0, dtype=scores.dtype)
        masked = jnp.where(adj > 0, scores, neg)
        attention = jax.nn.softmax(masked, axis=2)
        out_hid = jnp.matmul(attention, input)
        return out_hid
    h = jnp.maximum(_layernorm(x, axis=-1), 0.0)
    x = x + _L0_gnn_ref(h, adj, L0_gnn_W_msg, L0_gnn_W_upd, L0_gnn_bias)
    h = jnp.maximum(_layernorm(x, axis=-1), 0.0)
    x = x + _L1_gnn_ref(h, adj, L1_gnn_W, L1_gnn_b, L1_gnn_a)
    h = jnp.maximum(_layernorm(x, axis=-1), 0.0)
    x = x + _L2_gnn_ref(h, adj, L2_gnn_W1, L2_gnn_b1, L2_gnn_g1, L2_gnn_be1, L2_gnn_W2, L2_gnn_b2, L2_gnn_Wg, L2_gnn_bg, L2_gnn_gg, L2_gnn_beg, L2_gnn_Wt, L2_gnn_bt)
    h = jnp.maximum(_layernorm(x, axis=-1), 0.0)
    x = x + _L3_gnn_ref(h, adj)
    return x

_drawn_inputs = setup_inputs


def setup_inputs(seed=0):
    import zlib

    import numpy as np

    out = dict(_drawn_inputs(seed))
    spreads = {'L0_gnn_bias': (0.0, 0.1),
     'L1_gnn_b': (0.0, 0.1),
     'L2_gnn_b1': (0.0, 0.8),
     'L2_gnn_g1': (1.0, 0.54),
     'L2_gnn_be1': (0.0, 0.8),
     'L2_gnn_bg': (0.0, 0.8),
     'L2_gnn_gg': (1.0, 0.2),
     'L2_gnn_beg': (0.0, 0.1),
     'L2_gnn_bt': (0.0, 0.1)}
    factors = {}
    for name, (base, spread) in spreads.items():
        noise = np.random.default_rng([zlib.crc32(name.encode()), seed]).standard_normal(out[name].shape)
        drawn = base * np.exp(spread * noise) if base else spread * noise
        out[name] = jnp.asarray(drawn.astype(out[name].dtype))
    for name, factor in factors.items():
        out[name] = (out[name] * factor).astype(out[name].dtype)
    return out
```

```python
from contextlib import ExitStack

import concourse.bass as bass
from concourse import mybir

F32 = mybir.dt.float32
BF16 = mybir.dt.bfloat16
I32 = mybir.dt.int32
U32 = mybir.dt.uint32
ALU = mybir.AluOpType
ACT = mybir.ActivationFunctionType
AX_X = mybir.AxisListType.X

P = 128
B = 32
N = 256
F = 128
T = N // P
HEADS = 4
HD = F // HEADS
MID = 64
HALF = N // 2
GROUPS = 4
ROWS = P // GROUPS
STEPS = ROWS // 2
CHUNK = GROUPS * T * HALF
WRAP = N + HALF
RING = 4
NEG = -9.0e15
EPS = 1e-5
SCORE_SCALE = float(F) ** -0.5
ON_DVE = 3
PAIRS = float(B * N * N)


def wait(eng, sem, count):
    if not isinstance(count, int) or count > 0:
        eng.wait_ge(sem, count)


def sweep(eng, depth, body):
    first = depth + 2 + depth % 2
    for n in range(first):
        body(n, n % 2)
    with eng.Fori(first // 2, B // 2) as pair:
        body(pair * 2, 0)
        body(pair * 2 + 1, 1)
    for n in range(B, B + depth):
        body(n, n % 2)


def by_dve(k):
    return (k + 8 - ON_DVE) // 8


def has(b):
    return not isinstance(b, int) or 0 <= b < B


def build(nc, x, adj, w_msg, w_upd, bias0, w_l1, b_l1, a_l1, w1, b1, g1, be1, w2, b2, wg, bg, gg, beg, wt, bt, out):
    skew = nc.dram_tensor("skew", (T, P, N), F32, kind="Internal")
    with ExitStack() as ctx:
        def sb(name, shape, dt=F32):
            return ctx.enter_context(nc.sbuf_tensor(name, shape, dt))

        def sem(name):
            return ctx.enter_context(nc.semaphore(name))

        XR = sb("XR", [P, B * N])
        MN = sb("MN", [P, B * T * N], BF16)
        HT3 = sb("HT3", [P, B * WRAP])
        YG = sb("YG", [P, B * N])
        H = sb("H", [P, 2, T, F])
        HT = sb("HT", [P, 2, N])
        D = sb("D", [P, RING, 2, CHUNK])
        L = sb("L", [P, 2, CHUNK])
        AJ = D[:, 0, 0, :].bitcast(I32).rearrange("p (s n) -> p s n", s=2)
        A01 = D[:, 0, 1, :].rearrange("p (s n) -> p s n", s=2)
        ZM = D[:, 1, 0, 0:2 * T * (F + 1)].rearrange("p (s t f) -> p s t f", s=2, t=T)
        ZU = D[:, 1, 1, 0:2 * T * F].rearrange("p (s n) -> p s n", s=2)
        PR = D[:, 2, :, :]
        PTA = D[:, 3, :, :]
        V = L[:, 0, 0:2 * T * HEADS * (HD + 1)].rearrange("p (s t h d) -> p s t h d", s=2, t=T, h=HEADS)
        E8 = L[0:2 * HEADS, 1, 0:2 * N].rearrange("p (s n) -> p s n", s=2)
        TMP = L[:, 1, 2 * N:2 * N + 2 * F].rearrange("p (s n) -> p s n", s=2)
        SEL = YG[0:2 * HEADS, 0:2 * HEADS * N].rearrange("p (h j) -> p h j", h=2 * HEADS)
        WM = YG[:, 2048:2048 + 2 * F].rearrange("p (h d) -> p h d", d=HD)
        W01 = YG[:, 2304:2304 + 2 * F]
        B0 = YG[:, 2560:2560 + F]
        WL1 = YG[:, 2688:2688 + F]
        BL1 = YG[:, 2816:2816 + F]
        AB = YG[:, 2944:2944 + 2 * HD]
        WGN = YG[:, 3008:3008 + F]
        WTN = YG[:, 3136:3136 + 2 * F]
        BN = YG[:, 4096:4096 + B * 2 * 2 * 6]
        SD = YG[:, 5120:5120 + B * (STEPS - 2)]
        SQ = YG[:, 6144:6144 + B * (STEPS - 2)]
        SM = sb("SM", [P, 1, T * N])
        PT = sb("PT", [P, 1, T * N])
        SM3 = D[:, 0, 0, :].rearrange("p (s n) -> p s n", s=2)
        OUT = D[:, 1, 0, 0:2 * N].rearrange("p (s n) -> p s n", s=2)
        PT3 = D[:, 0, 1, :].rearrange("p (s n) -> p s n", s=2)
        SS = sb("SS", [P, N])
        U = sb("U", [P, T, N])
        YT = sb("YT", [P, N])
        ST = sb("ST", [P, B * T * 6])
        MS = sb("MS", [P, B * T])
        VA = sb("VA", [P, B * T])
        VB = sb("VB", [P, B * T])
        RSTD = sb("RSTD", [P, B * T])
        NBIAS = sb("NBIAS", [P, B * T])
        BY = sb("BY", [P, B * 6])
        MV = sb("MV", [P, 4])
        small = sb("small", [P, 64])
        mx = sb("mx", [P, 2, 8])
        rs = sb("rs", [P, 2, 8])
        ident = sb("ident", [P, P])
        eye0 = sb("eye0", [P, P])
        fold = sb("fold", [P, P])
        ones = sb("ones", [P, P])
        WA = sb("WA", [P, 2 * HEADS])
        CE = sb("CE", [P, 2 * HEADS])
        CE8 = sb("CE8", [2 * HEADS, 1])
        W1N = sb("W1N", [MID, F])
        W1T = sb("W1T", [P, 2 * MID])
        PC = sb("PC", [P, 16])
        W2P = sb("W2P", [P, 2 * ROWS])
        VP = sb("VP", [P, 2 * ROWS])
        WGT = sb("WGT", [P, F])
        WTT = sb("WTT", [P, 2, F])
        BTR = sb("BTR", [1, F])
        PS = [ctx.enter_context(nc.psum_tensor(f"PS{i}", [P, 512], F32)) for i in range(2)]
        PW = [ctx.enter_context(nc.psum_tensor(f"PW{i}", [P, 1024], F32)) for i in range(3)]

        B1, G1, BE1, W2C, B2C = (PC[:, i:i + 1] for i in range(5))
        BG, GG, BEG = (PC[:, i:i + 1] for i in range(5, 8))
        SCALE1, SHIFT1, C0, SC0 = (PC[:, i:i + 1] for i in range(8, 12))
        SCALEY, SHIFTY = PC[:, 12:13], PC[:, 13:14]

        def xr(b, t=None):
            return XR[:, bass.ds(b * N, N)] if t is None else XR[:, bass.ds(b * N + t * F, F)]

        def mn(b, t=None):
            return MN[:, bass.ds(b * T * N, T * N)] if t is None else MN[:, bass.ds(b * T * N + t * N, N)]

        X_LOADS = 4
        x_loaded = [sem(f"x_loaded{i}") for i in range(X_LOADS)]
        par_loaded = sem("par_loaded")
        adj_loaded = [sem(f"adj_loaded{i}") for i in range(2)]
        const_made = sem("const_made")
        prep_pe = sem("prep_pe")
        prep_v = sem("prep_v")
        vchain = sem("vchain")
        vstep = sem("vstep")
        astep = sem("astep")
        pstep = sem("pstep")
        ln_ready = sem("ln_ready")
        sd_ready = sem("sd_ready")
        sd_root = sem("sd_root")
        names = ["h", "t", "ht"]
        R = {}
        for lay in ("0", "1", "2", "3"):
            for nme in names:
                R[nme + lay] = sem(f"{nme}_ready{lay}")
        z0 = sem("z0_ready"); zm0 = sem("zm0_ready"); zu0 = sem("zu0_ready"); a01_ready = sem("a01_ready")
        agg0 = sem("agg0_ready"); deg0 = sem("deg0"); rdeg0 = sem("rdeg0"); o0 = sem("o0"); xr0 = sem("xr0"); st0 = sem("st0")
        ve1 = sem("ve1_ready"); v1 = sem("v1_ready"); z1 = sem("z1_ready"); zmask1 = sem("zmask1"); zl1 = sem("zl1"); mx1 = sem("mx1")
        p1 = sem("p1_ready"); pt1 = sem("pt1_ready"); ptc1 = sem("ptc1_ready"); o1 = sem("o1_ready")
        r1 = sem("r1"); n1 = sem("n1"); xr1 = sem("xr1"); st1 = sem("st1")
        ht3 = sem("ht3")
        diff_a = sem("diff_a"); absact_a = sem("absact_a"); absdve_a = sem("absdve_a"); pair_a = sem("pair_a")
        sq_a = sem("sq_a"); bn_a = sem("bn_a"); consts_b = sem("consts_b")
        diff_b = sem("diff_b"); abs_b = sem("abs_b"); pair_b = sem("pair_b"); relu_b = sem("relu_b"); score_b = sem("score_b")
        s_out = sem("s_out"); skewed = sem("skewed"); zeroed = sem("zeroed"); u_in = sem("u_in")
        full_b = sem("full_b"); mask_b = sem("mask_b"); max_b = sem("max_b"); exp_b = sem("exp_b"); rec_b = sem("rec_b")
        norm_b = sem("norm_b"); tr_b = sem("tr_b"); trc_b = sem("trc_b"); h_b = sem("h_b"); yt_b = sem("yt_b"); ytc_b = sem("ytc_b")
        yg_b = sem("yg_b"); ygs_b = sem("ygs_b"); by_b = sem("by_b")
        bn_y = sem("bn_y"); yl1 = sem("yl1"); yl2 = sem("yl2"); hx = sem("hx"); o2 = sem("o2"); xr2 = sem("xr2"); st2 = sem("st2")
        g3 = sem("g3"); m3 = sem("m3"); mx3 = sem("mx3"); ms3 = sem("ms3"); e3 = sem("e3"); tr3 = sem("tr3"); pt3 = sem("pt3"); av3 = sem("av3")
        rc3 = sem("rc3"); fin3 = sem("fin3"); stored = [sem(f"stored{i}") for i in range(2)]

        TILES = B * T
        IPARAMS = 0

        block = ctx.enter_context(nc.Block())

        params = [
            (W01[:, 0:F], w_msg), (W01[:, F:2 * F], w_upd), (WL1[:, :], w_l1),
            (B0[:, :], bias0.rearrange("(a f) -> a f", a=1).broadcast_to([P, F])),
            (BL1[:, :], b_l1.rearrange("(a f) -> a f", a=1).broadcast_to([P, F])),
            (AB[:, :], a_l1.rearrange("d a -> a d").broadcast_to([P, 2 * HD])),
            (W1N[:, :], w1), (WGN[:, :], wg), (WTN[:, :], wt),
            (BTR[:, :], bt.rearrange("(a f) -> a f", a=1)),
            (B2C, b2.rearrange("(a f) -> a f", a=1).broadcast_to([P, 1])),
            (BG, bg.rearrange("(p a) -> p a", a=1)), (GG, gg.rearrange("(p a) -> p a", a=1)),
            (BEG, beg.rearrange("(p a) -> p a", a=1)),
        ]
        for half in range(2):
            rows = slice(half * MID, (half + 1) * MID)
            params += [(PC[rows, 0:1], b1.rearrange("(p a) -> p a", a=1)),
                       (PC[rows, 1:2], g1.rearrange("(p a) -> p a", a=1)),
                       (PC[rows, 2:3], be1.rearrange("(p a) -> p a", a=1)),
                       (PC[rows, 3:4], w2.rearrange("a p -> p a"))]

        @block.sync
        def _(sp):
            per = B // X_LOADS
            for i in range(X_LOADS):
                src = x[i * per:(i + 1) * per].rearrange("b (t p) f -> p (b t) f", p=P)
                dst = XR[:, i * per * N:(i + 1) * per * N].rearrange("p (g f) -> p g f", f=F)
                sp.dma_start(dst, src).then_inc(x_loaded[i], 16)
                if i == 0:
                    for dst, src in params:
                        with nc.allow_non_contiguous_dma(reason="a few parameters"):
                            sp.dma_start(dst, src).then_inc(par_loaded, 16)

            def known(value):
                return value if isinstance(value, int) else sp.snap(value)

            def load_adj(b, s):
                start, used = known(b * (N * N)), known(b - 1)
                wait(sp, a01_ready, used)
                sp.dma_start(AJ[:, s, :].rearrange("p (t j) -> p t j", t=T),
                             bass.AP(adj.tensor, start, [[N, P], [P * N, T], [1, N]])).then_inc(adj_loaded[s], 16)
            for b in range(2):
                load_adj(b, b)
            with sp.Fori(1, B // 2) as pair:
                load_adj(pair * 2, 0)
                load_adj(pair * 2 + 1, 1)

            sp.wait_ge(zeroed, 1)
            sp.dma_start(skew[:, :, :].rearrange("t p j -> p t j"), U[:, :, :]).then_inc(skewed, 16)
            sp.wait_ge(skewed, 16)

            def bounce(b):
                sp.wait_ge(s_out, b + 1)
                sp.dma_start(bass.AP(skew, 1, [[N + 1, P], [1, HALF]]), SS[:, 0:HALF]).then_inc(skewed, 16)
                sp.dma_start(bass.AP(skew, P * N + 1, [[N + 1, P], [1, HALF - 1]]), SS[:, HALF + 1:N]).then_inc(skewed, 16)
                sp.wait_ge(skewed, b * 32 + 48)
                sp.dma_start(U[:, :, :], skew[:, :, :].rearrange("t p j -> p t j")).then_inc(u_in, 16)
            bounce(0)
            with sp.Fori(1, B) as b:
                bounce(b)

            def store(b, s):
                start, ready = known(b * (N * F)), known(b + 1)
                sp.wait_ge(fin3, ready)
                sp.dma_start(bass.AP(out.tensor, start, [[F, P], [P * F, T], [1, F]]),
                             OUT[:, s, :].rearrange("p (t f) -> p t f", t=T)).then_inc(stored[s], 16)
            with sp.Fori(0, B // 2) as pair:
                store(pair * 2, 0)
                store(pair * 2 + 1, 1)
            for s in range(2):
                sp.wait_ge(stored[s], 16 * (B // 2))

        @block.gpsimd
        def _(pool):
            pool.memset(ident[:, :], 0.0).then_inc(const_made, 1)
            pool.memset(fold[:, :], 0.0).then_inc(const_made, 1)
            pool.memset(SEL, 0.0).then_inc(const_made, 1)
            pool.wait_ge(const_made, 3)
            pool.affine_select(out=ident[:, :], in_=ident[:, :], compare_op=ALU.not_equal, fill=1.0,
                               base=0, pattern=[[-1, P]], channel_multiplier=1).then_inc(const_made, 1)
            for n, off in enumerate((0, MID, -MID)):
                pool.affine_select(out=fold[:, :], in_=fold[:, :], compare_op=ALU.not_equal, fill=1.0,
                                   base=off, pattern=[[-1, P]], channel_multiplier=1).then_inc(const_made, 1)
                pool.wait_ge(const_made, 5 + n)
            pool.affine_select(out=SEL, in_=SEL, compare_op=ALU.not_equal, fill=1.0,
                               base=0, pattern=[[-1, 2 * HEADS], [0, N]], channel_multiplier=1).then_inc(const_made, 1)
            pool.memset(ones[:, :], 1.0).then_inc(const_made, 1)

        @block.scalar
        def _(act):
            def root(n):
                act.wait_ge(sd_ready, n)
                act.activation(VA[:, :], VA[:, :], ACT.Sqrt).then_inc(sd_root, 1)

            def normalised(b, s, free, ready):
                wait(act, *free)
                for t in range(T):
                    ins = act.activation(H[:, s, t, :], xr(b, t), ACT.Relu,
                                         bias=NBIAS[:, bass.ds(b * T + t, 1)], scale=RSTD[:, bass.ds(b * T + t, 1)])
                ins.then_inc(ready, 1)

            root(1)
            act.wait_ge(ln_ready, 1)

            def layer0(n, u):
                if has(n):
                    normalised(n, u, (R["t0"], n - 1), R["h0"])
                b, s = n - 1, 1 - u
                if has(b):
                    act.wait_ge(z0, b + 1)
                    wait(act, agg0, b - 1)
                    act.activation(ZM[:, s, :, 0:F], PW[s][:, 0:T * F].rearrange("p (t f) -> p t f", t=T),
                                   ACT.Copy).then_inc(zm0, 1)
            sweep(act, 1, layer0)

            root(2)
            act.wait_ge(ln_ready, 2)

            def layer1(n, u):
                if has(n):
                    normalised(n, u, (R["t1"], n - 1), R["h1"])
                b, s = n - 2, u
                if has(b):
                    for t in range(T):
                        act.wait_ge(mx1, b * T + t + 1)
                        for h in range(HEADS):
                            cols = slice(h * N, (h + 1) * N)
                            ins = act.activation(PR[:, t, cols], PR[:, t, cols], ACT.Exp, bias=mx[:, t, h:h + 1])
                        ins.then_inc(p1, 1)
                    for t in range(T):
                        act.wait_ge(pt1, b * T + t + 1)
                        wait(act, o1, b * T + t - 1)
                        act.activation(PTA[:, t, :], PW[2][:, :], ACT.Copy).then_inc(ptc1, 1)
            sweep(act, 2, layer1)

            root(3)
            act.wait_ge(ln_ready, 3)

            def layer2(n, u):
                if has(n):
                    normalised(n, u, (R["t2"], n - 1), R["h2"])
            sweep(act, 0, layer2)

            def first_pass(b):
                seen = 0
                for k in range(STEPS):
                    n = b * STEPS + k
                    if k % 8 != ON_DVE:
                        act.wait_ge(diff_a, n + 1)
                        act.activation(D[:, k % RING, :, :], D[:, k % RING, :, :], ACT.Abs,
                                       accum_out=SD[:, bass.ds(b * (STEPS - 2) + seen, 1)]).then_inc(absact_a, 1)
                        seen += 1
                    if k > 0:
                        squares(b, k - 1)
                squares(b, STEPS - 1)

            def squares(b, k):
                if k % 8 == ON_DVE:
                    return
                i = k - by_dve(k)
                act.wait_ge(pair_a, b * STEPS + k + 1)
                act.activation(PW[k % 2][:, :], PW[k % 2][:, :], ACT.Square,
                               accum_out=SQ[:, bass.ds(b * (STEPS - 2) + i, 1)]).then_inc(sq_a, 1)
            with act.Fori(0, B) as b:
                first_pass(b)

            act.wait_ge(sd_ready, 4)
            act.activation(SCALE1, SCALE1, ACT.Sqrt).then_inc(sd_root, 1)
            act.wait_ge(consts_b, 1)

            def relus(b, k):
                n = b * STEPS + k
                act.wait_ge(pair_b, n + 1)
                wait(act, score_b, n - 1)
                act.activation(L[:, k % 2, :], PW[k % 2][:, :], ACT.Relu, bias=SHIFT1, scale=SCALE1).then_inc(relu_b, 1)

            def second_pass(b):
                for k in range(STEPS):
                    n = b * STEPS + k
                    act.wait_ge(diff_b, n + 1)
                    act.activation(D[:, k % RING, :, :], D[:, k % RING, :, :], ACT.Abs).then_inc(abs_b, 1)
                    if k > 0:
                        relus(b, k - 1)
                    act_tail(b - 1, k)
                relus(b, STEPS - 1)
                act.wait_ge(score_b, (b + 1) * STEPS)
                wait(act, skewed, b * 32 + 16 if not isinstance(b, int) or b > 0 else 0)
                act.activation(SS[:, :], PW[2][:, 0:N], ACT.Identity, bias=C0).then_inc(s_out, 1)

            def act_tail(b, k):
                if not has(b):
                    return
                if k == 6:
                    wait(act, yt_b, b)
                    for t in range(T):
                        ins = act.activation(H[:, 0, t, :], xr(b, t), ACT.Relu,
                                             bias=NBIAS[:, bass.ds(b * T + t, 1)], scale=RSTD[:, bass.ds(b * T + t, 1)])
                    ins.then_inc(h_b, 1)
                if k == 8:
                    act.wait_ge(max_b, b + 1)
                    for t in range(T):
                        ins = act.activation(SM[:, 0, t * N:(t + 1) * N], SM[:, 0, t * N:(t + 1) * N], ACT.Exp,
                                             bias=mx[:, 0, t:t + 1], accum_out=rs[:, 0, t:t + 1])
                    ins.then_inc(exp_b, 1)
                if k == 15:
                    act.wait_ge(yg_b, b + 1)
                    act.activation(YG[:, bass.ds(b * N, N)], PS[1][:, N:2 * N], ACT.Identity, bias=BG).then_inc(ygs_b, 1)
            second_pass(0)
            with act.Fori(1, B) as b:
                second_pass(b)
            for k in range(STEPS):
                act_tail(B - 1, k)
            act.wait_ge(sd_ready, 5)
            act.activation(SCALEY, SCALEY, ACT.Sqrt).then_inc(sd_root, 1)

            root(6)
            act.wait_ge(ln_ready, 4)

            def layer3(n, u):
                b, s = n - 2, u
                if has(b):
                    act.wait_ge(ms3, b + 1)
                    for t in range(T):
                        cols = slice(t * N, (t + 1) * N)
                        ins = act.activation(SM3[:, s, cols], SM3[:, s, cols], ACT.Exp, bias=mx[:, s, 2 + t:3 + t],
                                             scale=SCORE_SCALE, accum_out=rs[:, s, t:t + 1])
                    ins.then_inc(e3, 1)
                    act.wait_ge(tr3, b + 1)
                    wait(act, av3, b - 1)
                    act.activation(PT3[:, s, :], PS[1][:, :], ACT.Copy).then_inc(pt3, 1)
                if has(n):
                    normalised(n, u, (av3, n - 1), R["h3"])
            sweep(act, 2, layer3)

        @block.tensor
        def _(pe):
            pe.wait_ge(const_made, 9)
            pe.wait_ge(par_loaded, 16 * len(params))
            pe.transpose(PS[0][:, 0:MID], W1N[:, :], ident[0:MID, 0:MID])
            pe.transpose(PS[0][:, P:2 * P], WGN[:, :], ident[:, :])
            pe.transpose(PS[0][:, 2 * P:3 * P], WTN[:, 0:F], ident[:, :])
            pe.transpose(PS[0][:, 3 * P:4 * P], WTN[:, F:2 * F], ident[:, :]).then_inc(prep_pe, 1)
            pe.wait_ge(prep_v, 1)
            pe.matmul(PS[1][0:2 * HEADS, 0:1], CE[:, :], ones[:, 0:1], start=True, stop=True).then_inc(prep_pe, 1)
            pe.wait_ge(prep_v, 2)

            def transposes(b, s, bank, h_ready, t_ready):
                pe.wait_ge(h_ready, b + 1)
                for t in range(T):
                    ins = pe.transpose(bank[:, t * P:(t + 1) * P], H[:, s, t, :], ident[:, :])
                ins.then_inc(t_ready, 1)

            def layer0(n, u):
                if has(n):
                    wait(pe, R["ht0"], n - 1)
                    transposes(n, u, PS[u], R["h0"], R["t0"])
                b, s = n - 1, 1 - u
                if has(b):
                    pe.wait_ge(R["ht0"], b + 1)
                    wait(pe, zm0, b - 1)
                    wait(pe, zu0, b - 1)
                    for t in range(T):
                        lhsT = HT[:, s, t * P:(t + 1) * P]
                        pe.matmul(PW[s][:, t * F:(t + 1) * F], lhsT, W01[:, 0:F], start=True, stop=True)
                        ins = pe.matmul(PW[s][:, 512 + t * F:512 + (t + 1) * F], lhsT, W01[:, F:2 * F], start=True, stop=True)
                    ins.then_inc(z0, 1)
                b, s = n - 2, u
                if has(b):
                    pe.wait_ge(zm0, b + 1)
                    pe.wait_ge(a01_ready, b + 1)
                    wait(pe, o0, b - 1)
                    for jt in range(T):
                        for it in range(T):
                            ins = pe.matmul(PW[2][:, s * 512 + jt * N:s * 512 + jt * N + F + 1],
                                            A01[:, s, it * N + jt * P:it * N + (jt + 1) * P], ZM[:, s, it, :],
                                            start=it == 0, stop=it == T - 1)
                    ins.then_inc(agg0, 1)
            sweep(pe, 2, layer0)

            def layer1(n, u):
                if has(n):
                    wait(pe, v1, n)
                    transposes(n, u, PS[0], R["h1"], R["t1"])
                    pe.wait_ge(R["ht1"], n + 1)
                    for t in range(T):
                        pe.matmul(PS[0][:, N + t * F:N + (t + 1) * F], HT[:, u, t * P:(t + 1) * P], WL1[:, :],
                                  start=True, stop=True)
                    pe.matmul(PS[0][0:2 * HEADS, 0:N], WA[:, :], HT[:, u, :], start=True, stop=True).then_inc(ve1, 1)
                b, s = n - 1, 1 - u
                if has(b):
                    pe.wait_ge(v1, b + 1)
                    for t in range(T):
                        wait(pe, zmask1, (b - 1) * T + t + 1)
                        for h in range(HEADS):
                            dst = PW[t][:, h * N:(h + 1) * N]
                            pe.matmul(dst, E8[:, s, t * P:(t + 1) * P], SEL[:, h, :], start=True, stop=False)
                            ins = pe.matmul(dst, SEL[:, HEADS + h, 0:P], E8[:, s, :], start=False, stop=True)
                        ins.then_inc(z1, 1)
                b, s = n - 2, u
                if has(b):
                    for t in range(T):
                        pe.wait_ge(p1, b * T + t + 1)
                        wait(pe, ptc1, b * T + t)
                        for jt in range(T):
                            for h in range(HEADS):
                                ins = pe.transpose(PW[2][:, (jt * HEADS + h) * P:(jt * HEADS + h + 1) * P],
                                                   PR[:, t, h * N + jt * P:h * N + (jt + 1) * P], ident[:, :])
                        ins.then_inc(pt1, 1)
                    for t in range(T):
                        pe.wait_ge(ptc1, b * T + t + 1)
                        wait(pe, n1, b * T + t)
                        for h in range(HEADS):
                            for jt in range(T):
                                ins = pe.matmul(PS[1][:, h * (HD + 1):(h + 1) * (HD + 1)],
                                                PTA[:, t, (jt * HEADS + h) * P:(jt * HEADS + h + 1) * P],
                                                V[:, s, jt, h, :], start=jt == 0, stop=jt == T - 1)
                        ins.then_inc(o1, 1)
            sweep(pe, 2, layer1)

            def layer2(n, u):
                if has(n):
                    wait(pe, ht3, n - 1)
                    transposes(n, u, PS[u], R["h2"], R["t2"])
            sweep(pe, 0, layer2)

            def pair_matmuls(k):
                for c in range(2):
                    for half in range(2):
                        ins = pe.matmul(PW[k % 2][half * MID:(half + 1) * MID, c * 512:(c + 1) * 512], W1T[:, 0:MID],
                                        D[:, k % RING, half, c * 512:(c + 1) * 512], start=True, stop=True)
                return ins

            def first_pass(b):
                for k in range(STEPS):
                    n = b * STEPS + k
                    if k % 8 == ON_DVE:
                        pe.wait_ge(absdve_a, b * 2 + by_dve(k))
                    else:
                        pe.wait_ge(absact_a, b * (STEPS - 2) + k + 1 - by_dve(k))
                    j = k - 2
                    if j % 8 == ON_DVE:
                        wait(pe, bn_a, b * 2 + by_dve(j))
                    else:
                        wait(pe, sq_a, b * (STEPS - 2) + j + 1 - by_dve(j))
                    pair_matmuls(k).then_inc(pair_a, 1)
            first_pass(0)
            with pe.Fori(1, B) as b:
                first_pass(b)

            pe.wait_ge(vstep, 1)
            pe.matmul(PS[0][:, 0:1], W1T[:, :], small[:, 0:1], start=True, stop=False)
            pe.matmul(PS[0][:, 0:1], fold[:, :], small[:, 1:2], start=False, stop=True)
            pe.matmul(PS[0][:, 1:2], fold[:, :], small[:, 2:3], start=True, stop=True).then_inc(pstep, 1)
            pe.wait_ge(vstep, 2)
            pe.matmul(PS[0][:, 0:1], W1N[:, :], small[0:MID, 16:17], start=True, stop=True)
            pe.matmul(PS[0][:, 2:4], ones[0:MID, :], small[0:MID, 17:19], start=True, stop=True).then_inc(pstep, 1)
            pe.wait_ge(consts_b, 1)

            def score_matmuls(b, k):
                n = b * STEPS + k
                pe.wait_ge(relu_b, n + 1)
                if k == 0:
                    wait(pe, s_out, b)
                at = ROWS - 1 - 2 * k
                for g in range(GROUPS):
                    pe.matmul(PW[2][g * ROWS:(g + 1) * ROWS, 0:N], W2P[:, at:at + ROWS],
                              L[:, k % 2, g * N:(g + 1) * N], start=k == 0, stop=False)
                for half in range(2):
                    for g in range(GROUPS):
                        ins = pe.matmul(PW[2][g * ROWS:(g + 1) * ROWS, 0:N], VP[:, at - half:at - half + ROWS],
                                        D[:, k % RING, half, g * N:(g + 1) * N], start=False,
                                        stop=k == STEPS - 1 and half == 1)
                ins.then_inc(score_b, 1)

            def second_pass(b):
                for k in range(STEPS):
                    n = b * STEPS + k
                    pe.wait_ge(abs_b, n + 1)
                    wait(pe, relu_b, n - 1)
                    pair_matmuls(k).then_inc(pair_b, 1)
                    if k > 0:
                        score_matmuls(b, k - 1)
                    pe_tail(b - 1, k)
                score_matmuls(b, STEPS - 1)

            def pe_tail(b, k):
                if not has(b):
                    return
                if k == 5:
                    pe.wait_ge(u_in, (b + 1) * 16)
                    wait(pe, mask_b, b)
                    blocks = [(U[:, 0, 0:P], U[:, 0, 0:P], True), (U[:, 0, P:N], U[:, 1, P:N], False),
                              (U[:, 1, P:N], U[:, 0, P:N], False), (U[:, 1, 0:P], U[:, 1, 0:P], True)]
                    for i, (own, other, diagonal) in enumerate(blocks):
                        dst = PS[0][:, i * P:(i + 1) * P]
                        pe.matmul(dst, ident[:, :], own, start=True, stop=False)
                        ins = pe.matmul(dst, other, ident[:, :], start=False, stop=not diagonal)
                        if diagonal:
                            ins = pe.matmul(dst, ident[:, :], eye0[:, :], start=False, stop=True)
                    ins.then_inc(full_b, 1)
                if k == 11:
                    pe.wait_ge(norm_b, b + 1)
                    wait(pe, ygs_b, b)
                    for jt in range(T):
                        for it in range(T):
                            ins = pe.transpose(PS[1][:, jt * N + it * P:jt * N + (it + 1) * P],
                                               SM[:, 0, it * N + jt * P:it * N + (jt + 1) * P], ident[:, :])
                    ins.then_inc(tr_b, 1)
                if k == 13:
                    pe.wait_ge(trc_b, b + 1)
                    pe.wait_ge(h_b, b + 1)
                    for jt in range(T):
                        ins = pe.matmul(PS[1][:, 0:N], H[:, 0, jt, :], PT[:, 0, jt * N:(jt + 1) * N],
                                        start=jt == 0, stop=jt == T - 1)
                    ins.then_inc(yt_b, 1)
                if k == 14:
                    pe.wait_ge(ytc_b, b + 1)
                    pe.matmul(PS[1][:, N:2 * N], WGT[:, :], YT[:, :], start=True, stop=True).then_inc(yg_b, 1)
            second_pass(0)
            with pe.Fori(1, B) as b:
                second_pass(b)
            for k in range(STEPS):
                pe_tail(B - 1, k)

            def project(n, u):
                b, s = n - 1, 1 - u
                if has(b):
                    pe.wait_ge(yl2, b + 1)
                    pe.wait_ge(hx, b + 1)
                    wait(pe, xr2, b - 1)
                    for t in range(T):
                        dst = PS[s][:, t * F:(t + 1) * F]
                        cols = slice(t * P, (t + 1) * P)
                        pe.matmul(dst, HT[:, s, cols], WTT[:, 0, :], start=True, stop=False)
                        pe.matmul(dst, PT3[:, s, cols], WTT[:, 1, :], start=False, stop=False)
                        ins = pe.matmul(dst, ones[0:1, 0:P], BTR[:, :], start=False, stop=True)
                    ins.then_inc(o2, 1)
            sweep(pe, 1, project)

            def layer3(n, u):
                b, s = n - 2, u
                if has(b):
                    pe.wait_ge(e3, b + 1)
                    wait(pe, pt3, b)
                    for jt in range(T):
                        for it in range(T):
                            ins = pe.transpose(PS[1][:, jt * N + it * P:jt * N + (it + 1) * P],
                                               SM3[:, s, it * N + jt * P:it * N + (jt + 1) * P], ident[:, :])
                    ins.then_inc(tr3, 1)
                b, s = n - 1, 1 - u
                if has(b):
                    pe.wait_ge(R["ht3"], b + 1)
                    wait(pe, m3, b - 1)
                    for t in range(T):
                        ins = pe.matmul(PW[s][:, t * N:(t + 1) * N], HT[:, s, t * P:(t + 1) * P], HT[:, s, :],
                                        start=True, stop=True)
                    ins.then_inc(g3, 1)
                b, s = n - 2, u
                if has(b):
                    pe.wait_ge(pt3, b + 1)
                    wait(pe, fin3, b - 1)
                    for it in range(T):
                        for jt in range(T):
                            ins = pe.matmul(PW[2][:, s * 512 + it * F:s * 512 + (it + 1) * F],
                                            PT3[:, s, jt * N + it * P:jt * N + (it + 1) * P],
                                            H[:, s, jt, :], start=jt == 0, stop=jt == T - 1)
                    ins.then_inc(av3, 1)
                if has(n):
                    wait(pe, R["ht3"], n)
                    transposes(n, u, PS[0], R["h3"], R["t3"])
            sweep(pe, 2, layer3)

        @block.vector
        def _(dve):
            done = [0]

            def chain(ins):
                done[0] += 1
                ins.then_inc(own, 1)
                dve.wait_ge(own, done[0])

            own = vchain

            def ln_stats(b, ready_count_sem=None):
                for t in range(T):
                    ins = dve.bn_stats(ST[:, bass.ds((b * T + t) * 6, 6)], xr(b, t))
                return ins

            def ln_finish(n_root, n_ln):
                s = ST[:, :].rearrange("p (g k) -> p g k", k=6)
                chain(dve.tensor_tensor(MS[:, :], s[:, :, 1], s[:, :, 4], ALU.add))
                chain(dve.tensor_tensor(VB[:, :], s[:, :, 1], s[:, :, 4], ALU.subtract))
                chain(dve.tensor_tensor(VA[:, :], s[:, :, 2], s[:, :, 5], ALU.add))
                chain(dve.tensor_tensor(VB[:, :], VB[:, :], VB[:, :], ALU.mult))
                chain(dve.tensor_scalar(VA[:, :], VA[:, :], 1.0 / F, EPS, ALU.mult, ALU.add))
                dve.scalar_tensor_tensor(VA[:, :], VB[:, :], 0.25, VA[:, :], ALU.mult, ALU.add).then_inc(sd_ready, 1)
                dve.wait_ge(sd_root, n_root)
                chain(dve.reciprocal(RSTD[:, :], VA[:, :]))
                dve.scalar_tensor_tensor(NBIAS[:, :], MS[:, :], -0.5, RSTD[:, :], ALU.mult, ALU.mult).then_inc(ln_ready, 1)

            for i in range(X_LOADS):
                dve.wait_ge(x_loaded[i], 16)
                with dve.Fori(i * (B // X_LOADS), (i + 1) * (B // X_LOADS)) as b:
                    ins = ln_stats(b)
                    ins.then_inc(st0, 1)
            dve.wait_ge(st0, B)
            ln_finish(1, 1)

            chain(dve.memset(ZM[:, :, :, F:F + 1], 1.0))
            dve.wait_ge(par_loaded, 16 * len(params))
            ab = AB[:, :].rearrange("p (s d) -> p s d", s=2)
            for side in range(2):
                for h in range(HEADS):
                    dve.tensor_tensor(WM[:, side * HEADS + h, :], WL1[:, h * HD:(h + 1) * HD], ab[:, side, :], ALU.mult)
            chain(dve.tensor_copy(small[:, 63:64], B2C))
            chain(dve.tensor_reduce(WA[:, :], WM, AX_X, ALU.add))
            for side in range(2):
                for h in range(HEADS):
                    dve.tensor_tensor(WM[:, side * HEADS + h, :], BL1[:, h * HD:(h + 1) * HD], ab[:, side, :], ALU.mult)
            chain(dve.tensor_copy(small[:, 63:64], B2C))
            chain(dve.tensor_reduce(CE[:, :], WM, AX_X, ALU.add))
            dve.tensor_scalar(CE[:, :], CE[:, :], 1.0 / P, None, ALU.mult).then_inc(prep_v, 1)
            dve.wait_ge(prep_pe, 1)
            for half in range(2):
                dve.tensor_copy(W1T[:, half * MID:(half + 1) * MID], PS[0][:, 0:MID])
            dve.tensor_copy(WGT[:, :], PS[0][:, P:2 * P])
            dve.tensor_copy(WTT[:, :, :].rearrange("p a f -> p (a f)"), PS[0][:, 2 * P:4 * P])
            dve.wait_ge(prep_pe, 2)
            chain(dve.tensor_copy(CE8[:, :], PS[1][0:2 * HEADS, 0:1]))
            dve.tensor_copy(small[:, 63:64], B2C).then_inc(prep_v, 1)

            def transposed(b, s, bank, t_ready, ht_ready, free):
                dve.wait_ge(t_ready, b + 1)
                wait(dve, *free)
                dve.tensor_copy(HT[:, s, :], bank[:, 0:N]).then_inc(ht_ready, 1)

            def layer0(n, u):
                if has(n):
                    transposed(n, u, PS[u], R["t0"], R["ht0"], (z0, n - 1))
                    dve.wait_ge(adj_loaded[u], (n // 2) * 16 + 16 if isinstance(n, int) else (n - u) * 8 + 16)
                    dve.tensor_scalar(mn(n), AJ[:, u, :], 0.0, None, ALU.is_le)
                    wait(dve, agg0, n - 1)
                    dve.tensor_scalar(A01[:, u, :], AJ[:, u, :], 0.0, None, ALU.not_equal).then_inc(a01_ready, 1)
                b, s = n - 3, 1 - u
                if has(b):
                    dve.wait_ge(agg0, b + 1)
                    acc = PW[2][:, s * 512:s * 512 + T * N].rearrange("p (t f) -> p t f", t=T)
                    dve.tensor_scalar(rs[:, s, 0:T], acc[:, :, F], 1.0, None, ALU.max).then_inc(deg0, 1)
                    dve.wait_ge(deg0, b + 1)
                    dve.reciprocal(rs[:, s, 2:2 + T], rs[:, s, 0:T]).then_inc(rdeg0, 1)
                    dve.wait_ge(rdeg0, b + 1)
                    for t in range(T):
                        cols = slice(t * F, (t + 1) * F)
                        ins = dve.scalar_tensor_tensor(ZU[:, s, cols], acc[:, t, 0:F], rs[:, s, 2 + t:3 + t],
                                                       ZU[:, s, cols], ALU.mult, ALU.add)
                    ins.then_inc(o0, 1)
                    dve.wait_ge(o0, b + 1)
                    dve.scalar_tensor_tensor(xr(b), ZU[:, s, :], 0.0, xr(b), ALU.max, ALU.add).then_inc(xr0, 1)
                    dve.wait_ge(xr0, b + 1)
                    ln_stats(b).then_inc(st0, 1)
                b, s = n - 1, 1 - u
                if has(b):
                    dve.wait_ge(z0, b + 1)
                    wait(dve, o0, b - 1)
                    for t in range(T):
                        ins = dve.tensor_tensor(ZU[:, s, t * F:(t + 1) * F], PW[s][:, 512 + t * F:512 + (t + 1) * F],
                                                B0[:, :], ALU.add)
                    ins.then_inc(zu0, 1)
            sweep(dve, 3, layer0)
            dve.wait_ge(st0, 2 * B)
            ln_finish(2, 2)

            chain(dve.memset(V[:, :, :, :, HD:HD + 1], 1.0))
            bl1 = BL1[:, :].rearrange("p (h d) -> p h d", h=HEADS)

            def layer1(n, u):
                if has(n):
                    transposed(n, u, PS[0], R["t1"], R["ht1"], (ve1, n - 1))
                b, s = n - 1, 1 - u
                if has(b):
                    for t in range(T):
                        m = b * T + t
                        pr = PR[:, t, :].rearrange("p (h j) -> p h j", h=HEADS)
                        dve.wait_ge(z1, m + 1)
                        wait(dve, pt1, m - 1)
                        missing = mn(b, t).rearrange("p (a j) -> p a j", a=1).broadcast_to([P, HEADS, N])
                        dve.scalar_tensor_tensor(pr, missing, NEG, PW[t][:, :].rearrange("p (h j) -> p h j", h=HEADS),
                                                 ALU.mult, ALU.add).then_inc(zmask1, 1)
                        dve.wait_ge(zmask1, m + 1)
                        dve.scalar_tensor_tensor(pr, pr, 0.2, pr, ALU.mult, ALU.max).then_inc(zl1, 1)
                        dve.wait_ge(zl1, m + 1)
                        dve.tensor_reduce(mx[:, t, 0:HEADS], pr, AX_X, ALU.max, negate=True).then_inc(mx1, 1)
                b, s = n - 2, u
                if has(b):
                    for t in range(T):
                        m = b * T + t
                        dve.wait_ge(o1, m + 1)
                        o = PS[1][:, 0:HEADS * (HD + 1)].rearrange("p (h d) -> p h d", h=HEADS)
                        dve.reciprocal(rs[:, t, 0:HEADS], o[:, :, HD]).then_inc(r1, 1)
                        dve.wait_ge(r1, m + 1)
                        per_head = rs[:, t, 0:HEADS].rearrange("p (h a) -> p h a", a=1).broadcast_to([P, HEADS, HD])
                        dve.tensor_tensor(TMP[:, t, :].rearrange("p (h d) -> p h d", h=HEADS), o[:, :, 0:HD],
                                          per_head, ALU.mult).then_inc(n1, 1)
                        dve.wait_ge(n1, m + 1)
                        dve.tensor_tensor(xr(b, t), xr(b, t), TMP[:, t, :], ALU.add).then_inc(xr1, 1)
                        dve.wait_ge(xr1, m + 1)
                        dve.bn_stats(ST[:, bass.ds(m * 6, 6)], xr(b, t)).then_inc(st1, 1)
                if has(n):
                    dve.wait_ge(ve1, n + 1)
                    wait(dve, o1, (n - 1) * T)
                    for t in range(T):
                        dve.tensor_tensor(V[:, u, t, :, 0:HD],
                                          PS[0][:, N + t * F:N + (t + 1) * F].rearrange("p (h d) -> p h d", h=HEADS),
                                          bl1, ALU.add)
                    wait(dve, z1, (n - 1) * T)
                    dve.tensor_scalar(E8[:, u, :], PS[0][0:2 * HEADS, 0:N], CE8[:, :], None, ALU.add).then_inc(v1, 1)
            sweep(dve, 2, layer1)
            dve.wait_ge(st1, TILES)
            ln_finish(3, 3)

            def layer2(n, u):
                if has(n):
                    dve.wait_ge(R["t2"], n + 1)
                    dve.tensor_copy(HT3[:, bass.ds(n * WRAP, N)], PS[u][:, 0:N])
                    dve.tensor_copy(HT3[:, bass.ds(n * WRAP + N, HALF)], PS[u][:, 0:HALF]).then_inc(ht3, 1)
            sweep(dve, 0, layer2)
            dve.wait_ge(ht3, B)

            def differences(b, k):
                for half in range(2):
                    at = b * WRAP + 2 * k + half
                    ahead = bass.AP(HT3, at + 1, [[B * WRAP, P], [ROWS, GROUPS], [P - 1, T], [1, HALF]])
                    here = bass.AP(HT3, at, [[B * WRAP, P], [ROWS, GROUPS], [P, T], [0, HALF]])
                    ins = dve.tensor_tensor(D[:, k % RING, half, :].rearrange("p (g t d) -> p g t d", g=GROUPS, t=T),
                                            ahead, here, ALU.subtract)
                return ins

            def first_pass(b):
                for k in range(STEPS):
                    n = b * STEPS + k
                    wait(dve, pair_a, n - RING + 1)
                    differences(b, k).then_inc(diff_a, 1)
                    if k % 8 == ON_DVE:
                        dve.wait_ge(diff_a, n + 1)
                        bits = D[:, k % RING, :, :].bitcast(U32)
                        dve.tensor_scalar(bits, bits, 0x7FFFFFFF, None, ALU.bitwise_and).then_inc(absdve_a, 1)
                    if k % 8 == ON_DVE + 2:
                        m = b * 2 + k // 8
                        dve.wait_ge(pair_a, n - 1)
                        for c in range(2):
                            ins = dve.bn_stats(BN[:, bass.ds(m * 12 + c * 6, 6)], PW[ON_DVE % 2][:, c * 512:(c + 1) * 512])
                        ins.then_inc(bn_a, 1)
            first_pass(0)
            with dve.Fori(1, B) as b:
                first_pass(b)

            dve.wait_ge(absact_a, B * (STEPS - 2))
            dve.wait_ge(sq_a, B * (STEPS - 2))
            dve.wait_ge(bn_a, B * 2)
            sm = small
            bnv = BN.rearrange("p (g k) -> p g k", k=3)
            chain(dve.tensor_reduce(sm[:, 0:1], SD, AX_X, ALU.add))
            chain(dve.tensor_reduce(sm[:, 3:4], SQ, AX_X, ALU.add))
            chain(dve.tensor_reduce(sm[:, 4:5], bnv[:, :, 1], AX_X, ALU.add))
            chain(dve.tensor_reduce(sm[:, 5:6], bnv[:, :, 2], AX_X, ALU.add))
            chain(dve.tensor_tensor(bnv[:, :, 1], bnv[:, :, 1], bnv[:, :, 1], ALU.mult))
            chain(dve.tensor_reduce(sm[:, 6:7], bnv[:, :, 1], AX_X, ALU.add))
            half_bank = 256.0
            chain(dve.tensor_scalar(sm[:, 1:2], sm[:, 4:5], half_bank, None, ALU.mult))
            chain(dve.scalar_tensor_tensor(sm[:, 7:8], sm[:, 6:7], half_bank, sm[:, 5:6], ALU.mult, ALU.add))
            dve.tensor_tensor(sm[:, 2:3], sm[:, 7:8], sm[:, 3:4], ALU.add).then_inc(vstep, 1)
            dve.wait_ge(pstep, 1)
            chain(dve.tensor_scalar(sm[:, 8:10], PS[0][:, 0:2], 2.0 / PAIRS, None, ALU.mult))
            chain(dve.tensor_tensor(sm[:, 10:11], sm[:, 8:9], sm[:, 8:9], ALU.mult))
            chain(dve.tensor_tensor(sm[:, 11:12], sm[:, 9:10], sm[:, 10:11], ALU.subtract))
            dve.tensor_scalar(SCALE1, sm[:, 11:12], EPS, None, ALU.add).then_inc(sd_ready, 1)
            dve.wait_ge(sd_root, 4)
            chain(dve.reciprocal(sm[:, 12:13], SCALE1))
            chain(dve.tensor_tensor(SCALE1, sm[:, 12:13], G1, ALU.mult))
            chain(dve.tensor_tensor(sm[:, 13:14], sm[:, 8:9], B1, ALU.add))
            chain(dve.tensor_tensor(sm[:, 13:14], B1, sm[:, 13:14], ALU.subtract))
            chain(dve.scalar_tensor_tensor(SHIFT1, sm[:, 13:14], SCALE1, BE1, ALU.mult, ALU.add))
            chain(dve.tensor_scalar(sm[:, 14:15], W2C, 0.01, None, ALU.mult))
            chain(dve.tensor_scalar(sm[:, 15:16], W2C, 0.99, None, ALU.mult))
            chain(dve.tensor_tensor(sm[:, 16:17], sm[:, 14:15], SCALE1, ALU.mult))
            chain(dve.tensor_tensor(sm[:, 17:18], sm[:, 14:15], SHIFT1, ALU.mult))
            dve.scalar_tensor_tensor(sm[:, 18:19], SHIFT1, 0.0, sm[:, 15:16], ALU.max, ALU.mult).then_inc(vstep, 1)
            dve.memset(W2P[:, :], 0.0)
            chain(dve.memset(VP[:, :], 0.0))
            dve.memset(U[:, :, :], 0.0).then_inc(zeroed, 1)
            for half in range(2):
                rows = slice(half * MID, (half + 1) * MID)
                chain(dve.tensor_copy(W2P[rows, ROWS - 1 + half:ROWS + half], sm[rows, 15:16]))
            dve.wait_ge(pstep, 2)
            chain(dve.tensor_copy(VP[:, ROWS - 1:ROWS], PS[0][:, 0:1]))
            chain(dve.tensor_tensor(C0, PS[0][:, 2:3], B2C, ALU.add))
            chain(dve.tensor_tensor(SC0, PS[0][:, 3:4], C0, ALU.add))
            dve.tensor_scalar(eye0[:, :], ident[:, :], SC0, None, ALU.mult).then_inc(consts_b, 1)
            dve.wait_ge(zeroed, 1)

            def second_pass(b):
                for k in range(STEPS):
                    n = b * STEPS + k
                    wait(dve, score_b, n - RING + 1)
                    differences(b, k).then_inc(diff_b, 1)
                    dve_tail(b - 1, k)

            def dve_tail(b, k):
                if not has(b):
                    return
                if k == 7:
                    dve.wait_ge(full_b, b + 1)
                    wait(dve, tr_b, b)
                    dve.scalar_tensor_tensor(SM[:, 0, :], mn(b), NEG, PS[0][:, :], ALU.mult, ALU.add).then_inc(mask_b, 1)
                    dve.wait_ge(mask_b, b + 1)
                    dve.tensor_reduce(mx[:, 0, 0:T], SM[:, 0, :].rearrange("p (t j) -> p t j", t=T), AX_X, ALU.max,
                                      negate=True).then_inc(max_b, 1)
                if k == 10:
                    dve.wait_ge(exp_b, b + 1)
                    dve.reciprocal(rs[:, 0, 2:2 + T], rs[:, 0, 0:T]).then_inc(rec_b, 1)
                    dve.wait_ge(rec_b, b + 1)
                    for t in range(T):
                        cols = slice(t * N, (t + 1) * N)
                        ins = dve.tensor_scalar(SM[:, 0, cols], SM[:, 0, cols], rs[:, 0, 2 + t:3 + t], None, ALU.mult)
                    ins.then_inc(norm_b, 1)
                if k == 12:
                    dve.wait_ge(tr_b, b + 1)
                    wait(dve, yt_b, b)
                    dve.tensor_copy(PT[:, 0, :], PS[1][:, :]).then_inc(trc_b, 1)
                if k == 14:
                    dve.wait_ge(yt_b, b + 1)
                    wait(dve, yg_b, b)
                    dve.tensor_copy(YT[:, :], PS[1][:, 0:N]).then_inc(ytc_b, 1)
                if k == 15:
                    dve.wait_ge(ygs_b, b + 1)
                    dve.bn_stats(BY[:, bass.ds(b * 6, 6)], YG[:, bass.ds(b * N, N)]).then_inc(by_b, 1)
            second_pass(0)
            with dve.Fori(1, B) as b:
                second_pass(b)
            for k in range(STEPS):
                dve_tail(B - 1, k)
            dve.wait_ge(by_b, B)
            chain(dve.bn_aggr(MV[:, 0:2], BY[:, :].rearrange("p (g k) -> p g k", k=6)))
            dve.tensor_scalar(SCALEY, MV[:, 1:2], EPS, None, ALU.add).then_inc(sd_ready, 1)
            dve.wait_ge(sd_root, 5)
            chain(dve.reciprocal(MV[:, 2:3], SCALEY))
            chain(dve.tensor_tensor(SCALEY, MV[:, 2:3], GG, ALU.mult))
            chain(dve.tensor_tensor(MV[:, 3:4], MV[:, 0:1], SCALEY, ALU.mult))
            chain(dve.tensor_tensor(SHIFTY, BEG, MV[:, 3:4], ALU.subtract))

            def project(n, u):
                if has(n):
                    wait(dve, o2, n - 1)
                    dve.tensor_scalar(SM3[:, u, 0:N], YG[:, bass.ds(n * N, N)], SCALEY, SHIFTY, ALU.mult, ALU.add).then_inc(yl1, 1)
                    dve.tensor_copy(HT[:, u, :], HT3[:, bass.ds(n * WRAP, N)]).then_inc(hx, 1)
                    dve.wait_ge(yl1, n + 1)
                    dve.scalar_tensor_tensor(PT3[:, u, 0:N], SM3[:, u, 0:N], 0.01, SM3[:, u, 0:N], ALU.mult, ALU.max).then_inc(yl2, 1)
                b, s = n - 2, u
                if has(b):
                    dve.wait_ge(o2, b + 1)
                    dve.tensor_tensor(xr(b), xr(b), PS[s][:, 0:N], ALU.add).then_inc(xr2, 1)
                    dve.wait_ge(xr2, b + 1)
                    ln_stats(b).then_inc(st2, 1)
            sweep(dve, 2, project)
            dve.wait_ge(st2, B)
            ln_finish(6, 4)

            def layer3(n, u):
                b, s = n - 1, 1 - u
                if has(b):
                    dve.wait_ge(g3, b + 1)
                    wait(dve, tr3, b - 1)
                    dve.scalar_tensor_tensor(SM3[:, s, :], mn(b), NEG, PW[s][:, 0:T * N], ALU.mult, ALU.add).then_inc(m3, 1)
                    dve.wait_ge(m3, b + 1)
                    dve.tensor_reduce(mx[:, s, 0:T], SM3[:, s, :].rearrange("p (t j) -> p t j", t=T), AX_X, ALU.max,
                                      negate=True).then_inc(mx3, 1)
                    dve.wait_ge(mx3, b + 1)
                    dve.tensor_scalar(mx[:, s, 2:2 + T], mx[:, s, 0:T], SCORE_SCALE, None, ALU.mult).then_inc(ms3, 1)
                b, s = n - 2, u
                if has(b):
                    dve.wait_ge(av3, b + 1)
                    dve.reciprocal(rs[:, s, 2:2 + T], rs[:, s, 0:T]).then_inc(rc3, 1)
                    dve.wait_ge(rc3, b + 1)
                    if not isinstance(b, int) or b >= 2:
                        dve.wait_ge(stored[s], (b // 2) * 16 if isinstance(b, int) else (b - s) * 8)
                    for t in range(T):
                        ins = dve.scalar_tensor_tensor(OUT[:, s, t * F:(t + 1) * F],
                                                       PW[2][:, s * 512 + t * F:s * 512 + (t + 1) * F],
                                                       rs[:, s, 2 + t:3 + t], xr(b, t), ALU.mult, ALU.add)
                    ins.then_inc(fin3, 1)
                if has(n):
                    transposed(n, u, PS[0], R["t3"], R["ht3"], (g3, n - 1))
            sweep(dve, 2, layer3)


_INS = ['x', 'adj', 'L0_gnn_W_msg', 'L0_gnn_W_upd', 'L0_gnn_bias', 'L1_gnn_W', 'L1_gnn_b', 'L1_gnn_a',
        'L2_gnn_W1', 'L2_gnn_b1', 'L2_gnn_g1', 'L2_gnn_be1', 'L2_gnn_W2', 'L2_gnn_b2', 'L2_gnn_Wg', 'L2_gnn_bg',
        'L2_gnn_gg', 'L2_gnn_beg', 'L2_gnn_Wt', 'L2_gnn_bt']


def kernel(**inputs):
    import numpy as _np
    import concourse.bacc as _bacc
    from concourse import mybir as _mybir
    from concourse.bass_utils import run_bass_kernel_spmd as _run

    nc = _bacc.Bacc("TRN2", target_bir_lowering=False, num_devices=1)
    arrays, args = {}, []
    for name in _INS:
        a = _np.ascontiguousarray(inputs[name])
        arrays[f"in_{name}_dram"] = a
        args.append(nc.dram_tensor(f"in_{name}_dram", a.shape, _mybir.dt.from_np(a.dtype), kind="ExternalInput").ap())
    args.append(nc.dram_tensor("out_dram", (B, N, F), _mybir.dt.float32, kind="ExternalOutput").ap())
    build(nc, *args)
    r = _run(nc, [arrays], core_ids=[0])
    return r.results[0]["out_dram"]
```

```python
from contextlib import ExitStack

import concourse.bass as bass
from concourse import mybir

F32 = mybir.dt.float32
BF16 = mybir.dt.bfloat16
I32 = mybir.dt.int32
U32 = mybir.dt.uint32
ALU = mybir.AluOpType
ACT = mybir.ActivationFunctionType
AX_X = mybir.AxisListType.X

P = 128
B = 32
N = 256
F = 128
T = N // P
HEADS = 4
HD = F // HEADS
MID = 64
HALF = N // 2
GROUPS = 4
ROWS = P // GROUPS
STEPS = ROWS // 2
CHUNK = GROUPS * T * HALF
WRAP = N + HALF
RING = 4
PAIR_BANKS = 4
NEG = -9.0e15
EPS = 1e-5
SCORE_SCALE = float(F) ** -0.5
ON_DVE = 3
LINEAR_LAG = 3
BN_LAG = 4
SQ_LAG = 2
PAIRS = float(B * N * N)
S_OUT_AT, EXP_AT = 1, 9
FULL_AT, TR_AT, YT_AT, YG_AT = 6, 11, 13, 15
MASK_AT, NORM_AT, TRC_AT, YTC_AT, BY_AT = 9, 12, 14, 15, 4


def wait(eng, sem, count):
    if not isinstance(count, int) or count > 0:
        eng.wait_ge(sem, count)


def sweep(eng, depth, body):
    first = depth + 2 + depth % 2
    for n in range(first):
        body(n, n % 2)
    with eng.Fori(first // 2, B // 2) as pair:
        body(pair * 2, 0)
        body(pair * 2 + 1, 1)
    for n in range(B, B + depth):
        body(n, n % 2)


def by_dve(k):
    return (k + 8 - ON_DVE) // 8


def linear_by_dve(k):
    return k % 2 == 0


def linear_before(k):
    return (k + 1) // 2


def has(b):
    return not isinstance(b, int) or 0 <= b < B


def build(nc, x, adj, w_msg, w_upd, bias0, w_l1, b_l1, a_l1, w1, b1, g1, be1, w2, b2, wg, bg, gg, beg, wt, bt, out):
    skew = nc.dram_tensor("skew", (T, P, N), F32, kind="Internal")
    with ExitStack() as ctx:
        def sb(name, shape, dt=F32):
            return ctx.enter_context(nc.sbuf_tensor(name, shape, dt))

        def sem(name):
            return ctx.enter_context(nc.semaphore(name))

        XR = sb("XR", [P, B * N])
        MN = sb("MN", [P, B * T * N], BF16)
        HT3 = sb("HT3", [P, B * WRAP])
        YG = sb("YG", [P, B * N])
        H = sb("H", [P, 2, T, F])
        HT = sb("HT", [P, 2, N])
        D = sb("D", [P, RING, 2, CHUNK])
        L = sb("L", [P, 2, CHUNK])
        AJ = D[:, 0, 0, :].bitcast(I32).rearrange("p (s n) -> p s n", s=2)
        A01 = D[:, 0, 1, :].rearrange("p (s n) -> p s n", s=2)
        ZM = D[:, 1, 0, 0:2 * T * (F + 1)].rearrange("p (s t f) -> p s t f", s=2, t=T)
        ZU = D[:, 1, 1, 0:2 * T * F].rearrange("p (s n) -> p s n", s=2)
        PR = D[:, 0:2, :, :]
        PTA = D[:, 2:4, :, :]
        V = L[:, 0, 0:2 * T * HEADS * (HD + 1)].rearrange("p (s t h d) -> p s t h d", s=2, t=T, h=HEADS)
        TMP = L[:, 1, 0:N]
        EI = L[:, 1, N:N + 2 * T * HEADS].rearrange("p (s t h) -> p s t h", s=2, t=T)
        WJ = YG[:, 0:HEADS * P].rearrange("p (h i) -> p h i", h=HEADS)
        WV = YG[:, 1024:1024 + F + HEADS]
        BV = YG[0:1, 1280:1280 + F + HEADS]
        WM = YG[:, 2048:2048 + 2 * F].rearrange("p (h d) -> p h d", d=HD)
        W01 = YG[:, 2304:2304 + 2 * F]
        B0 = YG[:, 2560:2560 + F]
        WL1 = WV[:, 0:F]
        BL1 = YG[:, 2816:2816 + F]
        AB = YG[:, 2944:2944 + 2 * HD]
        WGN = YG[:, 3008:3008 + F]
        WTN = YG[:, 3136:3136 + 2 * F]
        BN = YG[:, 4096:4096 + B * 2 * 2 * 6]
        SD = YG[:, 5120:5120 + B * (STEPS - 2)]
        SQ = YG[:, 6144:6144 + B * (STEPS - 2)]
        SM = sb("SM", [P, 1, T * N])
        PT = sb("PT", [P, 1, T * N])
        SM3 = D[:, 0, 0, :].rearrange("p (s n) -> p s n", s=2)
        OUT = D[:, 1, 0, 0:2 * N].rearrange("p (s n) -> p s n", s=2)
        PT3 = D[:, 0, 1, :].rearrange("p (s n) -> p s n", s=2)
        SS = sb("SS", [P, N])
        U = sb("U", [P, T, N])
        YT = sb("YT", [P, N])
        ST = sb("ST", [P, B * T * 6])
        MS = sb("MS", [P, B * T])
        VA = sb("VA", [P, B * T])
        VB = sb("VB", [P, B * T])
        RSTD = sb("RSTD", [P, B * T])
        NBIAS = sb("NBIAS", [P, B * T])
        BY = sb("BY", [P, B * 6])
        MV = sb("MV", [P, 4])
        small = sb("small", [P, 64])
        mx = sb("mx", [P, 2, 8])
        rs = sb("rs", [P, 2, 8])
        ident = sb("ident", [P, P])
        eye0 = sb("eye0", [P, P])
        fold = sb("fold", [P, P])
        ones = sb("ones", [P, P])
        WA = sb("WA", [P, 2 * HEADS])
        CE = sb("CE", [P, 2 * HEADS])
        W1N = sb("W1N", [MID, F])
        W1T = sb("W1T", [P, 2 * MID])
        PC = sb("PC", [P, 16])
        W2P = sb("W2P", [P, 2 * ROWS])
        VP = sb("VP", [P, 2 * ROWS])
        WGT = sb("WGT", [P, F])
        WTT = sb("WTT", [P, 2, F])
        BTR = sb("BTR", [1, F])
        PSUM = ctx.enter_context(nc.psum_tensor("PSUM", [P, 4096], F32))
        PW = [PSUM[:, i * 1024:(i + 1) * 1024] for i in range(PAIR_BANKS)]
        PS = [PSUM[:, i * 512:(i + 1) * 512] for i in (6, 7)]

        B1, G1, BE1, W2C, B2C = (PC[:, i:i + 1] for i in range(5))
        BG, GG, BEG = (PC[:, i:i + 1] for i in range(5, 8))
        SCALE1, SHIFT1, C0, SC0 = (PC[:, i:i + 1] for i in range(8, 12))
        SCALEY, SHIFTY = PC[:, 12:13], PC[:, 13:14]
        SLIN = PC[:, 14:15]

        def xr(b, t=None):
            return XR[:, bass.ds(b * N, N)] if t is None else XR[:, bass.ds(b * N + t * F, F)]

        def mn(b, t=None):
            return MN[:, bass.ds(b * T * N, T * N)] if t is None else MN[:, bass.ds(b * T * N + t * N, N)]

        X_LOADS = 4
        x_loaded = [sem(f"x_loaded{i}") for i in range(X_LOADS)]
        par_loaded = sem("par_loaded")
        adj_loaded = [sem(f"adj_loaded{i}") for i in range(2)]
        const_made = sem("const_made")
        prep_pe = sem("prep_pe")
        prep_v = sem("prep_v")
        vchain = sem("vchain")
        vstep = sem("vstep")
        astep = sem("astep")
        pstep = sem("pstep")
        ln_ready = sem("ln_ready")
        sd_ready = sem("sd_ready")
        sd_root = sem("sd_root")
        names = ["h", "t", "ht"]
        R = {}
        for lay in ("0", "1", "2", "3"):
            for nme in names:
                R[nme + lay] = sem(f"{nme}_ready{lay}")
        z0 = sem("z0_ready"); zm0 = sem("zm0_ready"); zu0 = sem("zu0_ready"); a01_ready = sem("a01_ready")
        agg0 = sem("agg0_ready"); deg0 = sem("deg0"); rdeg0 = sem("rdeg0"); o0 = sem("o0"); xr0 = sem("xr0"); st0 = sem("st0")
        ve1 = sem("ve1_ready"); v1 = sem("v1_ready"); ej1 = sem("ej1_ready"); ei1 = sem("ei1_ready"); zmask1 = sem("zmask1"); zl1 = sem("zl1"); mx1 = sem("mx1")
        p1 = sem("p1_ready"); pt1 = sem("pt1_ready"); ptc1 = sem("ptc1_ready"); o1 = sem("o1_ready")
        r1 = sem("r1"); n1 = sem("n1"); xr1 = sem("xr1"); st1 = sem("st1")
        ht3 = sem("ht3")
        diff_a = sem("diff_a"); absact_a = sem("absact_a"); absdve_a = sem("absdve_a"); pair_a = sem("pair_a")
        sq_a = sem("sq_a"); bn_a = sem("bn_a"); consts_b = sem("consts_b")
        diff_b = sem("diff_b"); abs_b = sem("abs_b"); pair_b = sem("pair_b"); relu_b = sem("relu_b"); lin_b = sem("lin_b"); direct_b = sem("direct_b"); score_b = sem("score_b")
        s_out = sem("s_out"); skewed = sem("skewed"); zeroed = sem("zeroed"); u_in = sem("u_in")
        full_b = sem("full_b"); mask_b = sem("mask_b"); max_b = sem("max_b"); exp_b = sem("exp_b"); rec_b = sem("rec_b")
        norm_b = sem("norm_b"); tr_b = sem("tr_b"); trc_b = sem("trc_b"); h_b = sem("h_b"); yt_b = sem("yt_b"); ytc_b = sem("ytc_b")
        yg_b = sem("yg_b"); ygs_b = sem("ygs_b"); by_b = sem("by_b")
        bn_y = sem("bn_y"); yl1 = sem("yl1"); yl2 = sem("yl2"); hx = sem("hx"); o2 = sem("o2"); xr2 = sem("xr2"); st2 = sem("st2")
        g3 = sem("g3"); m3 = sem("m3"); mx3 = sem("mx3"); ms3 = sem("ms3"); e3 = sem("e3"); tr3 = sem("tr3"); pt3 = sem("pt3"); av3 = sem("av3")
        rc3 = sem("rc3"); fin3 = sem("fin3"); stored = [sem(f"stored{i}") for i in range(2)]

        TILES = B * T
        LINEARS = linear_before(STEPS)

        block = ctx.enter_context(nc.Block())

        params = [
            (W01[:, 0:F], w_msg), (W01[:, F:2 * F], w_upd), (WL1[:, :], w_l1),
            (B0[:, :], bias0.rearrange("(a f) -> a f", a=1).broadcast_to([P, F])),
            (BL1[:, :], b_l1.rearrange("(a f) -> a f", a=1).broadcast_to([P, F])),
            (AB[:, :], a_l1.rearrange("d a -> a d").broadcast_to([P, 2 * HD])),
            (W1N[:, :], w1), (WGN[:, :], wg), (WTN[:, :], wt),
            (BTR[:, :], bt.rearrange("(a f) -> a f", a=1)),
            (B2C, b2.rearrange("(a f) -> a f", a=1).broadcast_to([P, 1])),
            (BG, bg.rearrange("(p a) -> p a", a=1)), (GG, gg.rearrange("(p a) -> p a", a=1)),
            (BEG, beg.rearrange("(p a) -> p a", a=1)),
        ]
        for half in range(2):
            rows = slice(half * MID, (half + 1) * MID)
            params += [(PC[rows, 0:1], b1.rearrange("(p a) -> p a", a=1)),
                       (PC[rows, 1:2], g1.rearrange("(p a) -> p a", a=1)),
                       (PC[rows, 2:3], be1.rearrange("(p a) -> p a", a=1)),
                       (PC[rows, 3:4], w2.rearrange("a p -> p a"))]

        @block.sync
        def _(sp):
            per = B // X_LOADS
            for i in range(X_LOADS):
                src = x[i * per:(i + 1) * per].rearrange("b (t p) f -> p (b t) f", p=P)
                dst = XR[:, i * per * N:(i + 1) * per * N].rearrange("p (g f) -> p g f", f=F)
                sp.dma_start(dst, src).then_inc(x_loaded[i], 16)
                if i == 0:
                    for dst, src in params:
                        with nc.allow_non_contiguous_dma(reason="a few parameters"):
                            sp.dma_start(dst, src).then_inc(par_loaded, 16)

            def known(value):
                return value if isinstance(value, int) else sp.snap(value)

            def load_adj(b, s):
                start, used = known(b * (N * N)), known(b - 1)
                wait(sp, a01_ready, used)
                sp.dma_start(AJ[:, s, :].rearrange("p (t j) -> p t j", t=T),
                             bass.AP(adj.tensor, start, [[N, P], [P * N, T], [1, N]])).then_inc(adj_loaded[s], 16)
            for b in range(2):
                load_adj(b, b)
            with sp.Fori(1, B // 2) as pair:
                load_adj(pair * 2, 0)
                load_adj(pair * 2 + 1, 1)

            sp.wait_ge(zeroed, 1)
            sp.dma_start(skew[:, :, :].rearrange("t p j -> p t j"), U[:, :, :]).then_inc(skewed, 16)
            sp.wait_ge(skewed, 16)

            def bounce(b):
                sp.wait_ge(s_out, b + 1)
                sp.dma_start(bass.AP(skew, 1, [[N + 1, P], [1, HALF]]), SS[:, 0:HALF]).then_inc(skewed, 16)
                sp.dma_start(bass.AP(skew, P * N + 1, [[N + 1, P], [1, HALF - 1]]), SS[:, HALF + 1:N]).then_inc(skewed, 16)
                sp.wait_ge(skewed, b * 32 + 48)
                sp.dma_start(U[:, :, :], skew[:, :, :].rearrange("t p j -> p t j")).then_inc(u_in, 16)
            bounce(0)
            with sp.Fori(1, B) as b:
                bounce(b)

            def store(b, s):
                start, ready = known(b * (N * F)), known(b + 1)
                sp.wait_ge(fin3, ready)
                sp.dma_start(bass.AP(out.tensor, start, [[F, P], [P * F, T], [1, F]]),
                             OUT[:, s, :].rearrange("p (t f) -> p t f", t=T)).then_inc(stored[s], 16)
            with sp.Fori(0, B // 2) as pair:
                store(pair * 2, 0)
                store(pair * 2 + 1, 1)
            for s in range(2):
                sp.wait_ge(stored[s], 16 * (B // 2))

        @block.gpsimd
        def _(pool):
            pool.memset(ident[:, :], 0.0).then_inc(const_made, 1)
            pool.memset(fold[:, :], 0.0).then_inc(const_made, 1)
            pool.wait_ge(const_made, 2)
            pool.affine_select(out=ident[:, :], in_=ident[:, :], compare_op=ALU.not_equal, fill=1.0,
                               base=0, pattern=[[-1, P]], channel_multiplier=1).then_inc(const_made, 1)
            for n, off in enumerate((0, MID, -MID)):
                pool.affine_select(out=fold[:, :], in_=fold[:, :], compare_op=ALU.not_equal, fill=1.0,
                                   base=off, pattern=[[-1, P]], channel_multiplier=1).then_inc(const_made, 1)
                pool.wait_ge(const_made, 4 + n)
            pool.memset(ones[:, :], 1.0).then_inc(const_made, 1)

        @block.scalar
        def _(act):
            def root(n):
                act.wait_ge(sd_ready, n)
                act.activation(VA[:, :], VA[:, :], ACT.Sqrt).then_inc(sd_root, 1)

            def normalised(b, s, free, ready):
                wait(act, *free)
                for t in range(T):
                    ins = act.activation(H[:, s, t, :], xr(b, t), ACT.Relu,
                                         bias=NBIAS[:, bass.ds(b * T + t, 1)], scale=RSTD[:, bass.ds(b * T + t, 1)])
                ins.then_inc(ready, 1)

            root(1)
            act.wait_ge(ln_ready, 1)

            def layer0(n, u):
                if has(n):
                    normalised(n, u, (R["t0"], n - 1), R["h0"])
                b, s = n - 1, 1 - u
                if has(b):
                    act.wait_ge(z0, b + 1)
                    wait(act, agg0, b - 1)
                    act.activation(ZM[:, s, :, 0:F], PW[s][:, 0:T * F].rearrange("p (t f) -> p t f", t=T),
                                   ACT.Copy).then_inc(zm0, 1)
            sweep(act, 1, layer0)

            root(2)
            act.wait_ge(ln_ready, 2)

            def layer1(n, u):
                b, s = n - 4, u
                if has(b):
                    for t in range(T):
                        act.wait_ge(mx1, b * T + t + 1)
                        for h in range(HEADS):
                            cols = slice(h * N, (h + 1) * N)
                            ins = act.activation(PR[:, s, t, cols], PR[:, s, t, cols], ACT.Exp,
                                                 bias=mx[:, s, t * HEADS + h:t * HEADS + h + 1])
                        ins.then_inc(p1, 1)

                def transposed_out(t):
                    if has(b):
                        act.wait_ge(pt1, b * T + t + 1)
                        wait(act, o1, b - 1)
                        act.activation(PTA[:, s, t, :], PW[2][:, :], ACT.Copy).then_inc(ptc1, 1)
                both = PW[1][:, 512:512 + T * (F + HEADS)].rearrange("p (t f) -> p t f", t=T)
                if has(n - 3):
                    act.wait_ge(ve1, n - 2)
                    wait(act, o1, n - 4)
                    for t in range(T):
                        ins = act.activation(V[:, 1 - u, t, :, 0:HD],
                                             both[:, t, 0:F].rearrange("p (h d) -> p h d", h=HEADS), ACT.Copy)
                    ins.then_inc(v1, 1)
                transposed_out(0)
                if has(n):
                    normalised(n, u, (R["t1"], n - 1), R["h1"])
                if has(n - 1):
                    act.wait_ge(R["t1"], n)
                    wait(act, ej1, n - 2)
                    wait(act, ve1, n - 2)
                    act.activation(HT[:, 1 - u, :], PW[1][:, 0:N], ACT.Copy).then_inc(R["ht1"], 1)
                if has(n - 2):
                    act.wait_ge(ve1, n - 1)
                    wait(act, zmask1, (n - 3) * T)
                    act.activation(EI[:, u, :, :], both[:, :, F:F + HEADS], ACT.Copy).then_inc(ei1, 1)
                transposed_out(1)
            sweep(act, 4, layer1)

            root(3)
            act.wait_ge(ln_ready, 3)

            def layer2(n, u):
                if has(n):
                    normalised(n, u, (R["t2"], n - 1), R["h2"])
            sweep(act, 0, layer2)

            def first_pass(b):
                seen = 0
                for k in range(STEPS):
                    n = b * STEPS + k
                    if k % 8 != ON_DVE:
                        act.wait_ge(diff_a, n + 1)
                        act.activation(D[:, k % RING, :, :], D[:, k % RING, :, :], ACT.Abs,
                                       accum_out=SD[:, bass.ds(b * (STEPS - 2) + seen, 1)]).then_inc(absact_a, 1)
                        seen += 1
                    if k >= SQ_LAG:
                        squares(b, k - SQ_LAG)
                for k in range(STEPS - SQ_LAG, STEPS):
                    squares(b, k)

            def squares(b, k):
                if k % 8 == ON_DVE:
                    return
                i = k - by_dve(k)
                act.wait_ge(pair_a, b * STEPS + k + 1)
                act.activation(PW[k % PAIR_BANKS][:, :], PW[k % PAIR_BANKS][:, :], ACT.Square,
                               accum_out=SQ[:, bass.ds(b * (STEPS - 2) + i, 1)]).then_inc(sq_a, 1)
            with act.Fori(0, B) as b:
                first_pass(b)

            act.wait_ge(sd_ready, 4)
            act.activation(SCALE1, SCALE1, ACT.Sqrt).then_inc(sd_root, 1)
            act.wait_ge(consts_b, 1)

            def relus(b, k):
                n = b * STEPS + k
                act.wait_ge(pair_b, n + 1)
                wait(act, score_b, n - 1)
                act.activation(L[:, k % 2, :], PW[k % 2][:, :], ACT.Relu, bias=SHIFT1, scale=SCALE1).then_inc(relu_b, 1)

            def second_pass(b):
                for k in range(STEPS):
                    n = b * STEPS + k
                    act.wait_ge(diff_b, n + 1)
                    act.activation(D[:, k % RING, :, :], D[:, k % RING, :, :], ACT.Abs).then_inc(abs_b, 1)
                    if k > 0:
                        relus(b, k - 1)
                    elif has(b - 1):
                        relus(b - 1, STEPS - 1)
                    act_tail(b - 1, k)

            def act_tail(b, k):
                if k == 1 and has(b - 1):
                    act.wait_ge(yg_b, b)
                    act.activation(YG[:, bass.ds((b - 1) * N, N)], PS[1][:, N:2 * N], ACT.Identity, bias=BG).then_inc(ygs_b, 1)
                if not has(b):
                    return
                if k == S_OUT_AT:
                    act.wait_ge(score_b, (b + 1) * STEPS)
                    wait(act, skewed, b * 32 + 16 if not isinstance(b, int) or b > 0 else 0)
                    act.activation(SS[:, :], PW[2][:, 0:N], ACT.Identity, bias=C0).then_inc(s_out, 1)
                if k == 6:
                    wait(act, yt_b, b)
                    for t in range(T):
                        ins = act.activation(H[:, 0, t, :], xr(b, t), ACT.Relu,
                                             bias=NBIAS[:, bass.ds(b * T + t, 1)], scale=RSTD[:, bass.ds(b * T + t, 1)])
                    ins.then_inc(h_b, 1)
                if k == EXP_AT:
                    act.wait_ge(max_b, b + 1)
                    for t in range(T):
                        ins = act.activation(SM[:, 0, t * N:(t + 1) * N], SM[:, 0, t * N:(t + 1) * N], ACT.Exp,
                                             bias=mx[:, 0, t:t + 1], accum_out=rs[:, 0, t:t + 1])
                    ins.then_inc(exp_b, 1)
            second_pass(0)
            second_pass(1)
            with act.Fori(2, B) as b:
                second_pass(b)
            relus(B - 1, STEPS - 1)
            for b in (B - 1, B):
                for k in range(STEPS):
                    act_tail(b, k)
            act.wait_ge(sd_ready, 5)
            act.activation(SCALEY, SCALEY, ACT.Sqrt).then_inc(sd_root, 1)

            root(6)
            act.wait_ge(ln_ready, 4)

            def layer3(n, u):
                b, s = n - 2, u
                if has(b):
                    act.wait_ge(ms3, b + 1)
                    for t in range(T):
                        cols = slice(t * N, (t + 1) * N)
                        ins = act.activation(SM3[:, s, cols], SM3[:, s, cols], ACT.Exp, bias=mx[:, s, 2 + t:3 + t],
                                             scale=SCORE_SCALE, accum_out=rs[:, s, t:t + 1])
                    ins.then_inc(e3, 1)
                    act.wait_ge(tr3, b + 1)
                    wait(act, av3, b - 1)
                    act.activation(PT3[:, s, :], PS[1][:, :], ACT.Copy).then_inc(pt3, 1)
                if has(n):
                    normalised(n, u, (av3, n - 1), R["h3"])
            sweep(act, 2, layer3)

        @block.tensor
        def _(pe):
            pe.wait_ge(const_made, 7)
            pe.wait_ge(par_loaded, 16 * len(params))
            pe.transpose(PS[0][:, 0:MID], W1N[:, :], ident[0:MID, 0:MID])
            pe.transpose(PS[0][:, P:2 * P], WGN[:, :], ident[:, :])
            pe.transpose(PS[0][:, 2 * P:3 * P], WTN[:, 0:F], ident[:, :])
            pe.transpose(PS[0][:, 3 * P:4 * P], WTN[:, F:2 * F], ident[:, :]).then_inc(prep_pe, 1)
            pe.wait_ge(prep_v, 1)

            def transposes(b, s, bank, h_ready, t_ready):
                pe.wait_ge(h_ready, b + 1)
                for t in range(T):
                    ins = pe.transpose(bank[:, t * P:(t + 1) * P], H[:, s, t, :], ident[:, :])
                ins.then_inc(t_ready, 1)

            def layer0(n, u):
                if has(n):
                    wait(pe, R["ht0"], n - 1)
                    transposes(n, u, PS[u], R["h0"], R["t0"])
                b, s = n - 1, 1 - u
                if has(b):
                    pe.wait_ge(R["ht0"], b + 1)
                    wait(pe, zm0, b - 1)
                    wait(pe, zu0, b - 1)
                    for t in range(T):
                        lhsT = HT[:, s, t * P:(t + 1) * P]
                        pe.matmul(PW[s][:, t * F:(t + 1) * F], lhsT, W01[:, 0:F], start=True, stop=True)
                        ins = pe.matmul(PW[s][:, 512 + t * F:512 + (t + 1) * F], lhsT, W01[:, F:2 * F], start=True, stop=True)
                    ins.then_inc(z0, 1)
                b, s = n - 2, u
                if has(b):
                    pe.wait_ge(zm0, b + 1)
                    pe.wait_ge(a01_ready, b + 1)
                    wait(pe, o0, b - 1)
                    for jt in range(T):
                        for it in range(T):
                            ins = pe.matmul(PW[2][:, s * 512 + jt * N:s * 512 + jt * N + F + 1],
                                            A01[:, s, it * N + jt * P:it * N + (jt + 1) * P], ZM[:, s, it, :],
                                            start=it == 0, stop=it == T - 1)
                    ins.then_inc(agg0, 1)
            sweep(pe, 2, layer0)

            def layer1(n, u):
                b, s = n - 5, 1 - u
                if has(b):
                    pe.wait_ge(v1, b + 1)
                    wait(pe, n1, b - 1)
                    for t in range(T):
                        pe.wait_ge(ptc1, b * T + t + 1)
                        for h in range(HEADS):
                            for jt in range(T):
                                at = (t * HEADS + h) * (HD + 1)
                                ins = pe.matmul(PS[s][:, at:at + HD + 1],
                                                PTA[:, s, t, (jt * HEADS + h) * P:(jt * HEADS + h + 1) * P],
                                                V[:, s, jt, h, :], start=jt == 0, stop=jt == T - 1)
                    ins.then_inc(o1, 1)
                if has(n - 1):
                    wait(pe, R["ht1"], n - 1)
                    transposes(n - 1, 1 - u, PW[1], R["h1"], R["t1"])
                if has(n - 2):
                    wait(pe, v1, n - 2)
                    wait(pe, ei1, n - 2)
                    for t in range(T):
                        dst = PW[1][:, 512 + t * (F + HEADS):512 + (t + 1) * (F + HEADS)]
                        pe.matmul(dst, HT[:, u, t * P:(t + 1) * P], WV, start=True, stop=False)
                        ins = pe.matmul(dst, ones[0:1, 0:P], BV, start=False, stop=True)
                    ins.then_inc(ve1, 1)

                def transposed_probabilities(t):
                    b = n - 4
                    if has(b):
                        pe.wait_ge(p1, b * T + t + 1)
                        wait(pe, ptc1, b * T + t)
                        for jt in range(T):
                            for h in range(HEADS):
                                ins = pe.transpose(PW[2][:, (jt * HEADS + h) * P:(jt * HEADS + h + 1) * P],
                                                   PR[:, u, t, h * N + jt * P:h * N + (jt + 1) * P], ident[:, :])
                        ins.then_inc(pt1, 1)
                transposed_probabilities(0)
                transposed_probabilities(1)
                if has(n - 2):
                    pe.wait_ge(R["ht1"], n - 1)
                    wait(pe, zmask1, (n - 2) * T)
                    for h in range(HEADS):
                        ins = pe.matmul(PW[0][:, h * N:(h + 1) * N], WJ[:, h, :], HT[:, u, :], start=True, stop=True)
                    ins.then_inc(ej1, 1)
            sweep(pe, 5, layer1)

            def layer2(n, u):
                if has(n):
                    wait(pe, ht3, n - 1)
                    transposes(n, u, PS[u], R["h2"], R["t2"])
            sweep(pe, 0, layer2)

            def pair_matmuls(k, slots):
                for c in range(2):
                    for half in range(2):
                        ins = pe.matmul(PW[k % slots][half * MID:(half + 1) * MID, c * 512:(c + 1) * 512], W1T[:, 0:MID],
                                        D[:, k % RING, half, c * 512:(c + 1) * 512], start=True, stop=True)
                return ins

            def first_pass(b):
                for k in range(STEPS):
                    n = b * STEPS + k
                    if k % 8 == ON_DVE:
                        pe.wait_ge(absdve_a, b * 2 + by_dve(k))
                    else:
                        pe.wait_ge(absact_a, b * (STEPS - 2) + k + 1 - by_dve(k))
                    j = k - PAIR_BANKS
                    if j % 8 == ON_DVE:
                        wait(pe, bn_a, b * 2 + by_dve(j))
                    else:
                        wait(pe, sq_a, b * (STEPS - 2) + j + 1 - by_dve(j))
                    pair_matmuls(k, PAIR_BANKS).then_inc(pair_a, 1)
            first_pass(0)
            with pe.Fori(1, B) as b:
                first_pass(b)

            pe.wait_ge(vstep, 1)
            pe.matmul(PS[0][:, 0:1], W1T[:, :], small[:, 0:1], start=True, stop=False)
            pe.matmul(PS[0][:, 0:1], fold[:, :], small[:, 1:2], start=False, stop=True)
            pe.matmul(PS[0][:, 1:2], fold[:, :], small[:, 2:3], start=True, stop=True).then_inc(pstep, 1)
            pe.wait_ge(vstep, 2)
            pe.matmul(PS[0][:, 0:1], W1N[:, :], small[0:MID, 16:17], start=True, stop=True)
            pe.matmul(PS[0][:, 2:4], ones[0:MID, :], small[0:MID, 17:19], start=True, stop=True).then_inc(pstep, 1)
            pe.wait_ge(consts_b, 1)

            def score_matmuls(b, k):
                if linear_by_dve(k):
                    pe.wait_ge(lin_b, b * LINEARS + linear_before(k) + 1)
                else:
                    pe.wait_ge(relu_b, b * STEPS + k + 1)
                if k == 0:
                    wait(pe, s_out, b)
                at = ROWS - 1 - 2 * k
                for g in range(GROUPS):
                    ins = pe.matmul(PW[2][g * ROWS:(g + 1) * ROWS, 0:N], W2P[:, at:at + ROWS],
                                    L[:, k % 2, g * N:(g + 1) * N], start=k == 0, stop=k == STEPS - 1)
                ins.then_inc(score_b, 1)

            def linear_matmuls(k):
                at = ROWS - 1 - 2 * k
                for half in range(2):
                    for g in range(GROUPS):
                        ins = pe.matmul(PW[2][g * ROWS:(g + 1) * ROWS, 0:N], VP[:, at - half:at - half + ROWS],
                                        D[:, k % RING, half, g * N:(g + 1) * N], start=False, stop=False)
                ins.then_inc(direct_b, 1)

            def second_pass(b):
                for k in range(STEPS):
                    n = b * STEPS + k
                    pe.wait_ge(abs_b, n + 1)
                    if linear_by_dve(k - 2):
                        wait(pe, lin_b, b * LINEARS + linear_before(k - 2) + 1)
                    else:
                        wait(pe, relu_b, n - 1)
                    pair_matmuls(k, 2).then_inc(pair_b, 1)
                    if not linear_by_dve(k) and k > 1:
                        linear_matmuls(k)
                    if k > 0:
                        score_matmuls(b, k - 1)
                    elif has(b - 1):
                        score_matmuls(b - 1, STEPS - 1)
                    if k == 1:
                        linear_matmuls(k)
                    pe_tail(b - 1, k)

            def pe_tail(b, k):
                if not has(b):
                    return
                if k == FULL_AT:
                    pe.wait_ge(u_in, (b + 1) * 16)
                    wait(pe, mask_b, b)
                    blocks = [(U[:, 0, 0:P], U[:, 0, 0:P], True), (U[:, 0, P:N], U[:, 1, P:N], False),
                              (U[:, 1, P:N], U[:, 0, P:N], False), (U[:, 1, 0:P], U[:, 1, 0:P], True)]
                    for i, (own, other, diagonal) in enumerate(blocks):
                        dst = PS[0][:, i * P:(i + 1) * P]
                        pe.matmul(dst, ident[:, :], own, start=True, stop=False)
                        ins = pe.matmul(dst, other, ident[:, :], start=False, stop=not diagonal)
                        if diagonal:
                            ins = pe.matmul(dst, ident[:, :], eye0[:, :], start=False, stop=True)
                    ins.then_inc(full_b, 1)
                if k == TR_AT:
                    pe.wait_ge(norm_b, b + 1)
                    wait(pe, ygs_b, b)
                    for jt in range(T):
                        for it in range(T):
                            ins = pe.transpose(PS[1][:, jt * N + it * P:jt * N + (it + 1) * P],
                                               SM[:, 0, it * N + jt * P:it * N + (jt + 1) * P], ident[:, :])
                    ins.then_inc(tr_b, 1)
                if k == YT_AT:
                    pe.wait_ge(trc_b, b + 1)
                    pe.wait_ge(h_b, b + 1)
                    for jt in range(T):
                        ins = pe.matmul(PS[1][:, 0:N], H[:, 0, jt, :], PT[:, 0, jt * N:(jt + 1) * N],
                                        start=jt == 0, stop=jt == T - 1)
                    ins.then_inc(yt_b, 1)
                if k == YG_AT:
                    pe.wait_ge(ytc_b, b + 1)
                    pe.matmul(PS[1][:, N:2 * N], WGT[:, :], YT[:, :], start=True, stop=True).then_inc(yg_b, 1)
            second_pass(0)
            second_pass(1)
            with pe.Fori(2, B) as b:
                second_pass(b)
            score_matmuls(B - 1, STEPS - 1)
            for k in range(STEPS):
                pe_tail(B - 1, k)

            def project(n, u):
                b, s = n - 1, 1 - u
                if has(b):
                    pe.wait_ge(yl2, b + 1)
                    pe.wait_ge(hx, b + 1)
                    wait(pe, xr2, b - 1)
                    for t in range(T):
                        dst = PS[s][:, t * F:(t + 1) * F]
                        cols = slice(t * P, (t + 1) * P)
                        pe.matmul(dst, HT[:, s, cols], WTT[:, 0, :], start=True, stop=False)
                        pe.matmul(dst, PT3[:, s, cols], WTT[:, 1, :], start=False, stop=False)
                        ins = pe.matmul(dst, ones[0:1, 0:P], BTR[:, :], start=False, stop=True)
                    ins.then_inc(o2, 1)
            sweep(pe, 1, project)

            def layer3(n, u):
                b, s = n - 2, u
                if has(b):
                    pe.wait_ge(e3, b + 1)
                    wait(pe, pt3, b)
                    for jt in range(T):
                        for it in range(T):
                            ins = pe.transpose(PS[1][:, jt * N + it * P:jt * N + (it + 1) * P],
                                               SM3[:, s, it * N + jt * P:it * N + (jt + 1) * P], ident[:, :])
                    ins.then_inc(tr3, 1)
                b, s = n - 1, 1 - u
                if has(b):
                    pe.wait_ge(R["ht3"], b + 1)
                    wait(pe, m3, b - 1)
                    for t in range(T):
                        ins = pe.matmul(PW[s][:, t * N:(t + 1) * N], HT[:, s, t * P:(t + 1) * P], HT[:, s, :],
                                        start=True, stop=True)
                    ins.then_inc(g3, 1)
                b, s = n - 2, u
                if has(b):
                    pe.wait_ge(pt3, b + 1)
                    wait(pe, fin3, b - 1)
                    for it in range(T):
                        for jt in range(T):
                            ins = pe.matmul(PW[2][:, s * 512 + it * F:s * 512 + (it + 1) * F],
                                            PT3[:, s, jt * N + it * P:jt * N + (it + 1) * P],
                                            H[:, s, jt, :], start=jt == 0, stop=jt == T - 1)
                    ins.then_inc(av3, 1)
                if has(n):
                    wait(pe, R["ht3"], n)
                    transposes(n, u, PS[0], R["h3"], R["t3"])
            sweep(pe, 2, layer3)

        @block.vector
        def _(dve):
            done = [0]

            def chain(ins):
                done[0] += 1
                ins.then_inc(own, 1)
                dve.wait_ge(own, done[0])

            own = vchain

            def ln_stats(b, ready_count_sem=None):
                for t in range(T):
                    ins = dve.bn_stats(ST[:, bass.ds((b * T + t) * 6, 6)], xr(b, t))
                return ins

            def ln_finish(n_root, n_ln):
                s = ST[:, :].rearrange("p (g k) -> p g k", k=6)
                chain(dve.tensor_tensor(MS[:, :], s[:, :, 1], s[:, :, 4], ALU.add))
                chain(dve.tensor_tensor(VB[:, :], s[:, :, 1], s[:, :, 4], ALU.subtract))
                chain(dve.tensor_tensor(VA[:, :], s[:, :, 2], s[:, :, 5], ALU.add))
                chain(dve.tensor_tensor(VB[:, :], VB[:, :], VB[:, :], ALU.mult))
                chain(dve.tensor_scalar(VA[:, :], VA[:, :], 1.0 / F, EPS, ALU.mult, ALU.add))
                dve.scalar_tensor_tensor(VA[:, :], VB[:, :], 0.25, VA[:, :], ALU.mult, ALU.add).then_inc(sd_ready, 1)
                dve.wait_ge(sd_root, n_root)
                chain(dve.reciprocal(RSTD[:, :], VA[:, :]))
                dve.scalar_tensor_tensor(NBIAS[:, :], MS[:, :], -0.5, RSTD[:, :], ALU.mult, ALU.mult).then_inc(ln_ready, 1)

            for i in range(X_LOADS):
                dve.wait_ge(x_loaded[i], 16)
                with dve.Fori(i * (B // X_LOADS), (i + 1) * (B // X_LOADS)) as b:
                    ins = ln_stats(b)
                    ins.then_inc(st0, 1)
            dve.wait_ge(st0, B)
            ln_finish(1, 1)

            chain(dve.memset(ZM[:, :, :, F:F + 1], 1.0))
            dve.wait_ge(par_loaded, 16 * len(params))
            ab = AB[:, :].rearrange("p (s d) -> p s d", s=2)
            for side in range(2):
                for h in range(HEADS):
                    dve.tensor_tensor(WM[:, side * HEADS + h, :], WL1[:, h * HD:(h + 1) * HD], ab[:, side, :], ALU.mult)
            chain(dve.tensor_copy(small[:, 63:64], B2C))
            chain(dve.tensor_reduce(WA[:, :], WM, AX_X, ALU.add))
            for side in range(2):
                for h in range(HEADS):
                    dve.tensor_tensor(WM[:, side * HEADS + h, :], BL1[:, h * HD:(h + 1) * HD], ab[:, side, :], ALU.mult)
            chain(dve.tensor_copy(small[:, 63:64], B2C))
            chain(dve.tensor_reduce(CE[:, :], WM, AX_X, ALU.add))
            chain(dve.tensor_tensor(BV[:, F:F + HEADS], CE[0:1, 0:HEADS], CE[0:1, HEADS:2 * HEADS], ALU.add))
            dve.tensor_copy(BV[:, 0:F], BL1[0:1, :])
            dve.tensor_copy(WV[:, F:F + HEADS], WA[:, 0:HEADS])
            dve.tensor_copy(WJ, WA[:, HEADS:2 * HEADS].rearrange("p (h a) -> p h a", a=1).broadcast_to([P, HEADS, P]))
            dve.wait_ge(prep_pe, 1)
            for half in range(2):
                dve.tensor_copy(W1T[:, half * MID:(half + 1) * MID], PS[0][:, 0:MID])
            dve.tensor_copy(WGT[:, :], PS[0][:, P:2 * P])
            dve.tensor_copy(WTT[:, :, :].rearrange("p a f -> p (a f)"), PS[0][:, 2 * P:4 * P]).then_inc(prep_v, 1)

            def transposed(b, s, bank, t_ready, ht_ready, free):
                dve.wait_ge(t_ready, b + 1)
                wait(dve, *free)
                dve.tensor_copy(HT[:, s, :], bank[:, 0:N]).then_inc(ht_ready, 1)

            def layer0(n, u):
                if has(n):
                    transposed(n, u, PS[u], R["t0"], R["ht0"], (z0, n - 1))
                    dve.wait_ge(adj_loaded[u], (n // 2) * 16 + 16 if isinstance(n, int) else (n - u) * 8 + 16)
                    dve.tensor_scalar(mn(n), AJ[:, u, :], 0.0, NEG, ALU.is_le, ALU.mult)
                    wait(dve, agg0, n - 1)
                    dve.tensor_scalar(A01[:, u, :], AJ[:, u, :], 0.0, None, ALU.not_equal).then_inc(a01_ready, 1)
                b, s = n - 3, 1 - u
                if has(b):
                    dve.wait_ge(agg0, b + 1)
                    acc = PW[2][:, s * 512:s * 512 + T * N].rearrange("p (t f) -> p t f", t=T)
                    dve.tensor_scalar(rs[:, s, 0:T], acc[:, :, F], 1.0, None, ALU.max).then_inc(deg0, 1)
                    dve.wait_ge(deg0, b + 1)
                    dve.reciprocal(rs[:, s, 2:2 + T], rs[:, s, 0:T]).then_inc(rdeg0, 1)
                    dve.wait_ge(rdeg0, b + 1)
                    for t in range(T):
                        cols = slice(t * F, (t + 1) * F)
                        ins = dve.scalar_tensor_tensor(ZU[:, s, cols], acc[:, t, 0:F], rs[:, s, 2 + t:3 + t],
                                                       ZU[:, s, cols], ALU.mult, ALU.add)
                    ins.then_inc(o0, 1)
                    dve.wait_ge(o0, b + 1)
                    dve.scalar_tensor_tensor(xr(b), ZU[:, s, :], 0.0, xr(b), ALU.max, ALU.add).then_inc(xr0, 1)
                    dve.wait_ge(xr0, b + 1)
                    ln_stats(b).then_inc(st0, 1)
                b, s = n - 1, 1 - u
                if has(b):
                    dve.wait_ge(z0, b + 1)
                    wait(dve, o0, b - 1)
                    for t in range(T):
                        ins = dve.tensor_tensor(ZU[:, s, t * F:(t + 1) * F], PW[s][:, 512 + t * F:512 + (t + 1) * F],
                                                B0[:, :], ALU.add)
                    ins.then_inc(zu0, 1)
            sweep(dve, 3, layer0)
            dve.wait_ge(st0, 2 * B)
            ln_finish(2, 2)

            chain(dve.memset(V[:, :, :, :, HD:HD + 1], 1.0))

            def layer1(n, u):
                b, s = n - 3, 1 - u
                if has(b):
                    dve.wait_ge(ej1, b + 1)
                    dve.wait_ge(ei1, b + 1)
                    wait(dve, pt1, (b - 1) * T)
                    for t in range(T):
                        for h in range(HEADS):
                            cols = slice(h * N, (h + 1) * N)
                            ins = dve.scalar_tensor_tensor(PR[:, s, t, cols], PW[0][:, cols], EI[:, s, t, h:h + 1],
                                                           mn(b, t), ALU.add, ALU.add)
                        ins.then_inc(zmask1, 1)
                    for t in range(T):
                        dve.wait_ge(zmask1, b * T + t + 1)
                        dve.scalar_tensor_tensor(PR[:, s, t, :], PR[:, s, t, :], 0.2, PR[:, s, t, :], ALU.mult,
                                                 ALU.max).then_inc(zl1, 1)
                    for t in range(T):
                        dve.wait_ge(zl1, b * T + t + 1)
                        dve.tensor_reduce(mx[:, s, t * HEADS:(t + 1) * HEADS],
                                          PR[:, s, t, :].rearrange("p (h j) -> p h j", h=HEADS), AX_X, ALU.max,
                                          negate=True).then_inc(mx1, 1)
                b, s = n - 5, 1 - u
                if has(b):
                    dve.wait_ge(o1, b + 1)
                    o = PS[s][:, 0:T * HEADS * (HD + 1)].rearrange("p (h d) -> p h d", d=HD + 1)
                    dve.reciprocal(rs[:, s, :], o[:, :, HD]).then_inc(r1, 1)
                    dve.wait_ge(r1, b + 1)
                    per_head = rs[:, s, :].rearrange("p (h a) -> p h a", a=1).broadcast_to([P, T * HEADS, HD])
                    dve.tensor_tensor(TMP.rearrange("p (h d) -> p h d", d=HD), o[:, :, 0:HD], per_head,
                                      ALU.mult).then_inc(n1, 1)
                    dve.wait_ge(n1, b + 1)
                    dve.tensor_tensor(xr(b), xr(b), TMP, ALU.add).then_inc(xr1, 1)
                    dve.wait_ge(xr1, b + 1)
                    ln_stats(b).then_inc(st1, 1)
            sweep(dve, 5, layer1)
            dve.wait_ge(st1, B)
            ln_finish(3, 3)

            def layer2(n, u):
                if has(n):
                    dve.wait_ge(R["t2"], n + 1)
                    dve.tensor_copy(HT3[:, bass.ds(n * WRAP, N)], PS[u][:, 0:N])
                    dve.tensor_copy(HT3[:, bass.ds(n * WRAP + N, HALF)], PS[u][:, 0:HALF]).then_inc(ht3, 1)
            sweep(dve, 0, layer2)
            dve.wait_ge(ht3, B)

            def differences(b, k, halves=(0, 1)):
                for half in halves:
                    at = b * WRAP + 2 * k + half
                    ahead = bass.AP(HT3, at + 1, [[B * WRAP, P], [ROWS, GROUPS], [P - 1, T], [1, HALF]])
                    here = bass.AP(HT3, at, [[B * WRAP, P], [ROWS, GROUPS], [P, T], [0, HALF]])
                    ins = dve.tensor_tensor(D[:, k % RING, half, :].rearrange("p (g t d) -> p g t d", g=GROUPS, t=T),
                                            ahead, here, ALU.subtract)
                return ins

            def first_pass(b):
                for k in range(STEPS):
                    n = b * STEPS + k
                    wait(dve, pair_a, n - RING + 1)
                    differences(b, k).then_inc(diff_a, 1)
                    if k % 8 == ON_DVE:
                        dve.wait_ge(diff_a, n + 1)
                        bits = D[:, k % RING, :, :].bitcast(U32)
                        dve.tensor_scalar(bits, bits, 0x7FFFFFFF, None, ALU.bitwise_and).then_inc(absdve_a, 1)
                    if k % 8 == ON_DVE + BN_LAG:
                        m = b * 2 + k // 8
                        dve.wait_ge(pair_a, n - BN_LAG + 1)
                        for c in range(2):
                            ins = dve.bn_stats(BN[:, bass.ds(m * 12 + c * 6, 6)], PW[ON_DVE % PAIR_BANKS][:, c * 512:(c + 1) * 512])
                        ins.then_inc(bn_a, 1)
            first_pass(0)
            with dve.Fori(1, B) as b:
                first_pass(b)

            dve.wait_ge(absact_a, B * (STEPS - 2))
            dve.wait_ge(sq_a, B * (STEPS - 2))
            dve.wait_ge(bn_a, B * 2)
            sm = small
            bnv = BN.rearrange("p (g k) -> p g k", k=3)
            chain(dve.tensor_reduce(sm[:, 0:1], SD, AX_X, ALU.add))
            chain(dve.tensor_reduce(sm[:, 3:4], SQ, AX_X, ALU.add))
            chain(dve.tensor_reduce(sm[:, 4:5], bnv[:, :, 1], AX_X, ALU.add))
            chain(dve.tensor_reduce(sm[:, 5:6], bnv[:, :, 2], AX_X, ALU.add))
            chain(dve.tensor_tensor(bnv[:, :, 1], bnv[:, :, 1], bnv[:, :, 1], ALU.mult))
            chain(dve.tensor_reduce(sm[:, 6:7], bnv[:, :, 1], AX_X, ALU.add))
            half_bank = 256.0
            chain(dve.tensor_scalar(sm[:, 1:2], sm[:, 4:5], half_bank, None, ALU.mult))
            chain(dve.scalar_tensor_tensor(sm[:, 7:8], sm[:, 6:7], half_bank, sm[:, 5:6], ALU.mult, ALU.add))
            dve.tensor_tensor(sm[:, 2:3], sm[:, 7:8], sm[:, 3:4], ALU.add).then_inc(vstep, 1)
            dve.wait_ge(pstep, 1)
            chain(dve.tensor_scalar(sm[:, 8:10], PS[0][:, 0:2], 2.0 / PAIRS, None, ALU.mult))
            chain(dve.tensor_tensor(sm[:, 10:11], sm[:, 8:9], sm[:, 8:9], ALU.mult))
            chain(dve.tensor_tensor(sm[:, 11:12], sm[:, 9:10], sm[:, 10:11], ALU.subtract))
            dve.tensor_scalar(SCALE1, sm[:, 11:12], EPS, None, ALU.add).then_inc(sd_ready, 1)
            dve.wait_ge(sd_root, 4)
            chain(dve.reciprocal(sm[:, 12:13], SCALE1))
            chain(dve.tensor_tensor(SCALE1, sm[:, 12:13], G1, ALU.mult))
            chain(dve.tensor_scalar(SLIN, SCALE1, 0.01 / 0.99, None, ALU.mult))
            chain(dve.tensor_tensor(sm[:, 13:14], sm[:, 8:9], B1, ALU.add))
            chain(dve.tensor_tensor(sm[:, 13:14], B1, sm[:, 13:14], ALU.subtract))
            chain(dve.scalar_tensor_tensor(SHIFT1, sm[:, 13:14], SCALE1, BE1, ALU.mult, ALU.add))
            chain(dve.tensor_scalar(sm[:, 14:15], W2C, 0.01, None, ALU.mult))
            chain(dve.tensor_scalar(sm[:, 15:16], W2C, 0.99, None, ALU.mult))
            chain(dve.tensor_tensor(sm[:, 16:17], sm[:, 14:15], SCALE1, ALU.mult))
            chain(dve.tensor_tensor(sm[:, 17:18], sm[:, 14:15], SHIFT1, ALU.mult))
            dve.scalar_tensor_tensor(sm[:, 18:19], SHIFT1, 0.0, sm[:, 15:16], ALU.max, ALU.mult).then_inc(vstep, 1)
            dve.memset(W2P[:, :], 0.0)
            chain(dve.memset(VP[:, :], 0.0))
            dve.memset(U[:, :, :], 0.0).then_inc(zeroed, 1)
            for half in range(2):
                rows = slice(half * MID, (half + 1) * MID)
                chain(dve.tensor_copy(W2P[rows, ROWS - 1 + half:ROWS + half], sm[rows, 15:16]))
            dve.wait_ge(pstep, 2)
            chain(dve.tensor_copy(VP[:, ROWS - 1:ROWS], PS[0][:, 0:1]))
            chain(dve.tensor_tensor(C0, PS[0][:, 2:3], B2C, ALU.add))
            chain(dve.tensor_tensor(SC0, PS[0][:, 3:4], C0, ALU.add))
            dve.tensor_scalar(eye0[:, :], ident[:, :], SC0, None, ALU.mult).then_inc(consts_b, 1)
            dve.wait_ge(zeroed, 1)

            def second_pass(b):
                for k in range(STEPS):
                    n = b * STEPS + k
                    if linear_by_dve(k - RING):
                        wait(dve, pair_b, n - RING + 1)
                    else:
                        wait(dve, direct_b, b * (STEPS - LINEARS) + k - RING + 1 - linear_before(k - RING))
                    differences(b, k, [0])
                    if k >= LINEAR_LAG:
                        linear(b, k - LINEAR_LAG)
                    elif has(b - 1):
                        linear(b - 1, k - LINEAR_LAG + STEPS)
                    differences(b, k, [1]).then_inc(diff_b, 1)
                    dve_tail(b - 1, k)

            def linear(b, k):
                if not linear_by_dve(k):
                    return
                dve.wait_ge(relu_b, b * STEPS + k + 1)
                dve.scalar_tensor_tensor(L[:, k % 2, :], PW[k % 2][:, :], SLIN, L[:, k % 2, :], ALU.mult,
                                         ALU.add).then_inc(lin_b, 1)

            def dve_tail(b, k):
                if k == BY_AT and has(b - 1):
                    dve.wait_ge(ygs_b, b)
                    dve.bn_stats(BY[:, bass.ds((b - 1) * 6, 6)], YG[:, bass.ds((b - 1) * N, N)]).then_inc(by_b, 1)
                if not has(b):
                    return
                if k == MASK_AT:
                    dve.wait_ge(full_b, b + 1)
                    wait(dve, tr_b, b)
                    dve.tensor_tensor(SM[:, 0, :], PS[0][:, :], mn(b), ALU.add).then_inc(mask_b, 1)
                    dve.wait_ge(mask_b, b + 1)
                    dve.tensor_reduce(mx[:, 0, 0:T], SM[:, 0, :].rearrange("p (t j) -> p t j", t=T), AX_X, ALU.max,
                                      negate=True).then_inc(max_b, 1)
                if k == NORM_AT:
                    dve.wait_ge(exp_b, b + 1)
                    dve.reciprocal(rs[:, 0, 2:2 + T], rs[:, 0, 0:T]).then_inc(rec_b, 1)
                    dve.wait_ge(rec_b, b + 1)
                    for t in range(T):
                        cols = slice(t * N, (t + 1) * N)
                        ins = dve.tensor_scalar(SM[:, 0, cols], SM[:, 0, cols], rs[:, 0, 2 + t:3 + t], None, ALU.mult)
                    ins.then_inc(norm_b, 1)
                if k == TRC_AT:
                    dve.wait_ge(tr_b, b + 1)
                    wait(dve, yt_b, b)
                    dve.tensor_copy(PT[:, 0, :], PS[1][:, :]).then_inc(trc_b, 1)
                if k == YTC_AT:
                    dve.wait_ge(yt_b, b + 1)
                    wait(dve, yg_b, b)
                    dve.tensor_copy(YT[:, :], PS[1][:, 0:N]).then_inc(ytc_b, 1)
            second_pass(0)
            second_pass(1)
            with dve.Fori(2, B) as b:
                second_pass(b)
            for k in range(STEPS - LINEAR_LAG, STEPS):
                linear(B - 1, k)
            for b in (B - 1, B):
                for k in range(STEPS):
                    dve_tail(b, k)
            dve.wait_ge(by_b, B)
            chain(dve.bn_aggr(MV[:, 0:2], BY[:, :].rearrange("p (g k) -> p g k", k=6)))
            dve.tensor_scalar(SCALEY, MV[:, 1:2], EPS, None, ALU.add).then_inc(sd_ready, 1)
            dve.wait_ge(sd_root, 5)
            chain(dve.reciprocal(MV[:, 2:3], SCALEY))
            chain(dve.tensor_tensor(SCALEY, MV[:, 2:3], GG, ALU.mult))
            chain(dve.tensor_tensor(MV[:, 3:4], MV[:, 0:1], SCALEY, ALU.mult))
            chain(dve.tensor_tensor(SHIFTY, BEG, MV[:, 3:4], ALU.subtract))

            def project(n, u):
                if has(n):
                    wait(dve, o2, n - 1)
                    dve.tensor_scalar(SM3[:, u, 0:N], YG[:, bass.ds(n * N, N)], SCALEY, SHIFTY, ALU.mult, ALU.add).then_inc(yl1, 1)
                    dve.tensor_copy(HT[:, u, :], HT3[:, bass.ds(n * WRAP, N)]).then_inc(hx, 1)
                    dve.wait_ge(yl1, n + 1)
                    dve.scalar_tensor_tensor(PT3[:, u, 0:N], SM3[:, u, 0:N], 0.01, SM3[:, u, 0:N], ALU.mult, ALU.max).then_inc(yl2, 1)
                b, s = n - 2, u
                if has(b):
                    dve.wait_ge(o2, b + 1)
                    dve.tensor_tensor(xr(b), xr(b), PS[s][:, 0:N], ALU.add).then_inc(xr2, 1)
                    dve.wait_ge(xr2, b + 1)
                    ln_stats(b).then_inc(st2, 1)
            sweep(dve, 2, project)
            dve.wait_ge(st2, B)
            ln_finish(6, 4)

            def layer3(n, u):
                b, s = n - 1, 1 - u
                if has(b):
                    dve.wait_ge(g3, b + 1)
                    wait(dve, tr3, b - 1)
                    dve.tensor_tensor(SM3[:, s, :], PW[s][:, 0:T * N], mn(b), ALU.add).then_inc(m3, 1)
                    dve.wait_ge(m3, b + 1)
                    dve.tensor_reduce(mx[:, s, 0:T], SM3[:, s, :].rearrange("p (t j) -> p t j", t=T), AX_X, ALU.max,
                                      negate=True).then_inc(mx3, 1)
                    dve.wait_ge(mx3, b + 1)
                    dve.tensor_scalar(mx[:, s, 2:2 + T], mx[:, s, 0:T], SCORE_SCALE, None, ALU.mult).then_inc(ms3, 1)
                b, s = n - 2, u
                if has(b):
                    dve.wait_ge(av3, b + 1)
                    dve.reciprocal(rs[:, s, 2:2 + T], rs[:, s, 0:T]).then_inc(rc3, 1)
                    dve.wait_ge(rc3, b + 1)
                    if not isinstance(b, int) or b >= 2:
                        dve.wait_ge(stored[s], (b // 2) * 16 if isinstance(b, int) else (b - s) * 8)
                    for t in range(T):
                        ins = dve.scalar_tensor_tensor(OUT[:, s, t * F:(t + 1) * F],
                                                       PW[2][:, s * 512 + t * F:s * 512 + (t + 1) * F],
                                                       rs[:, s, 2 + t:3 + t], xr(b, t), ALU.mult, ALU.add)
                    ins.then_inc(fin3, 1)
                if has(n):
                    transposed(n, u, PS[0], R["t3"], R["ht3"], (g3, n - 1))
            sweep(dve, 2, layer3)


_INS = ['x', 'adj', 'L0_gnn_W_msg', 'L0_gnn_W_upd', 'L0_gnn_bias', 'L1_gnn_W', 'L1_gnn_b', 'L1_gnn_a',
        'L2_gnn_W1', 'L2_gnn_b1', 'L2_gnn_g1', 'L2_gnn_be1', 'L2_gnn_W2', 'L2_gnn_b2', 'L2_gnn_Wg', 'L2_gnn_bg',
        'L2_gnn_gg', 'L2_gnn_beg', 'L2_gnn_Wt', 'L2_gnn_bt']


def kernel(**inputs):
    import numpy as _np
    import concourse.bacc as _bacc
    from concourse import mybir as _mybir
    from concourse.bass_utils import run_bass_kernel_spmd as _run

    nc = _bacc.Bacc("TRN2", target_bir_lowering=False, num_devices=1)
    arrays, args = {}, []
    for name in _INS:
        a = _np.ascontiguousarray(inputs[name])
        arrays[f"in_{name}_dram"] = a
        args.append(nc.dram_tensor(f"in_{name}_dram", a.shape, _mybir.dt.from_np(a.dtype), kind="ExternalInput").ap())
    args.append(nc.dram_tensor("out_dram", (B, N, F), _mybir.dt.float32, kind="ExternalOutput").ap())
    build(nc, *args)
    r = _run(nc, [arrays], core_ids=[0])
    return r.results[0]["out_dram"]
```

```python
from contextlib import ExitStack

import concourse.bass as bass
from concourse import mybir

F32 = mybir.dt.float32
BF16 = mybir.dt.bfloat16
I32 = mybir.dt.int32
ALU = mybir.AluOpType
ACT = mybir.ActivationFunctionType
AX_X = mybir.AxisListType.X

P = 128
B = 32
N = 256
F = 128
T = N // P
HEADS = 4
HD = F // HEADS
MID = 64
HALF = N // 2
GROUPS = 4
ROWS = P // GROUPS
STEPS = ROWS // 2
CHUNK = GROUPS * T * HALF
WRAP = N + HALF
RING = 4
PAIR_BANKS = 4
NEG = -9.0e15
EPS = 1e-5
SCORE_SCALE = float(F) ** -0.5
KEPT = STEPS // 2
MADE = STEPS - KEPT
KEPT_SLOTS = 2
SQ_LAG = 3
KEEP_LAG = 3
LINEAR_LAG = 4
PAIRS = float(B * N * N)
BOUNCE_AT = 2
S_OUT_AT, EXP_AT, YG_OUT_AT = 1, 10, 4
FULL_AT, TR_AT, YT_AT, YG_AT = 6, 12, 14, 2
MASK_AT, NORM_AT, TRC_AT, YTC_AT, BY_AT = 11, 14, 1, 3, 8


def wait(eng, sem, count):
    if not isinstance(count, int) or count > 0:
        eng.wait_ge(sem, count)


def sweep(eng, depth, body):
    first = depth + 2 + depth % 2
    for n in range(first):
        body(n, n % 2)
    with eng.Fori(first // 2, B // 2) as pair:
        body(pair * 2, 0)
        body(pair * 2 + 1, 1)
    for n in range(B, B + depth):
        body(n, n % 2)


def is_kept(k):
    return k % 2 == 0


def has(b):
    return not isinstance(b, int) or 0 <= b < B


def build(nc, x, adj, w_msg, w_upd, bias0, w_l1, b_l1, a_l1, w1, b1, g1, be1, w2, b2, wg, bg, gg, beg, wt, bt, out):
    skew = nc.dram_tensor("skew", (T, P, N), F32, kind="Internal")
    kept = nc.dram_tensor("kept", (B * KEPT, P, CHUNK), F32, kind="Internal")
    with ExitStack() as ctx:
        def sb(name, shape, dt=F32):
            return ctx.enter_context(nc.sbuf_tensor(name, shape, dt))

        def sem(name):
            return ctx.enter_context(nc.semaphore(name))

        XR = sb("XR", [P, B * N])
        MN = sb("MN", [P, B * T * N], BF16)
        HT3 = sb("HT3", [P, B * WRAP])
        YG = sb("YG", [P, B * N])
        H = sb("H", [P, 2, T, F])
        HT = sb("HT", [P, 2, N])
        D = sb("D", [P, RING, 2, CHUNK])
        L = sb("L", [P, 2, CHUNK])
        K = sb("K", [P, KEPT_SLOTS, CHUNK])
        AJ = D[:, 0, 0, :].bitcast(I32).rearrange("p (s n) -> p s n", s=2)
        A01 = D[:, 0, 1, :].rearrange("p (s n) -> p s n", s=2)
        ZM = D[:, 1, 0, 0:2 * T * (F + 1)].rearrange("p (s t f) -> p s t f", s=2, t=T)
        ZU = D[:, 1, 1, 0:2 * T * F].rearrange("p (s n) -> p s n", s=2)
        PR = D[:, 0:2, :, :]
        PTA = D[:, 2:4, :, :]
        V = L[:, 0, 0:2 * T * HEADS * (HD + 1)].rearrange("p (s t h d) -> p s t h d", s=2, t=T, h=HEADS)
        TMP = L[:, 1, 0:N]
        EI = L[:, 1, N:N + 2 * T * HEADS].rearrange("p (s t h) -> p s t h", s=2, t=T)
        WJ = YG[:, 0:HEADS * P].rearrange("p (h i) -> p h i", h=HEADS)
        WV = YG[:, 1024:1024 + F + HEADS]
        BV = YG[0:1, 1280:1280 + F + HEADS]
        WM = YG[:, 2048:2048 + 2 * F].rearrange("p (h d) -> p h d", d=HD)
        W01 = YG[:, 2304:2304 + 2 * F]
        B0 = YG[:, 2560:2560 + F]
        WL1 = WV[:, 0:F]
        BL1 = YG[:, 2816:2816 + F]
        AB = YG[:, 2944:2944 + 2 * HD]
        WGN = YG[:, 3008:3008 + F]
        WTN = YG[:, 3136:3136 + 2 * F]
        SD = YG[:, 5120:5120 + B * STEPS]
        SQ = YG[:, 6144:6144 + B * STEPS]
        SM = sb("SM", [P, 1, T * N])
        PT = sb("PT", [P, 1, T * N])
        SM3 = D[:, 0, 0, :].rearrange("p (s n) -> p s n", s=2)
        OUT = D[:, 1, 0, 0:2 * N].rearrange("p (s n) -> p s n", s=2)
        PT3 = D[:, 0, 1, :].rearrange("p (s n) -> p s n", s=2)
        SS = HT[:, 0, :]
        YT = HT[:, 1, :]
        STATS = sb("STATS", [P, B * T * 8])
        ST = STATS[:, 0:B * T * 6]
        MS = STATS[:, B * T * 6:B * T * 7]
        VB = STATS[:, B * T * 7:B * T * 8]
        U = STATS[:, :].rearrange("p (t j) -> p t j", t=T)
        VA = HT[:, 0, 0:B * T]
        RSTD = sb("RSTD", [P, B * T])
        NBIAS = sb("NBIAS", [P, B * T])
        BY = sb("BY", [P, B * 6])
        MV = sb("MV", [P, 4])
        small = sb("small", [P, 64])
        mx = sb("mx", [P, 2, 8])
        rs = sb("rs", [P, 2, 8])
        ident = sb("ident", [P, P])
        eye0 = H[:, 1, 0, :]
        fold = YG[:, 7168:7168 + P]
        ones = sb("ones", [P, P])
        WA = sb("WA", [P, 2 * HEADS])
        CE = sb("CE", [P, 2 * HEADS])
        W1N = YG[0:MID, 7424:7424 + F]
        W1T = sb("W1T", [P, 2 * MID])
        PC = sb("PC", [P, 16])
        W2P = sb("W2P", [P, 2 * ROWS])
        VP = sb("VP", [P, 2 * ROWS])
        WGT = sb("WGT", [P, F])
        WTT = sb("WTT", [P, 2, F])
        BTR = sb("BTR", [1, F])
        PSUM = ctx.enter_context(nc.psum_tensor("PSUM", [P, 4096], F32))
        PW = [PSUM[:, i * 1024:(i + 1) * 1024] for i in range(PAIR_BANKS)]
        PS = [PSUM[:, i * 512:(i + 1) * 512] for i in (6, 7)]

        B1, G1, BE1, W2C, B2C = (PC[:, i:i + 1] for i in range(5))
        BG, GG, BEG = (PC[:, i:i + 1] for i in range(5, 8))
        SCALE1, SHIFT1, C0, SC0 = (PC[:, i:i + 1] for i in range(8, 12))
        SCALEY, SHIFTY = PC[:, 12:13], PC[:, 13:14]
        SLIN = PC[:, 14:15]

        def xr(b, t=None):
            return XR[:, bass.ds(b * N, N)] if t is None else XR[:, bass.ds(b * N + t * F, F)]

        def mn(b, t=None):
            return MN[:, bass.ds(b * T * N, T * N)] if t is None else MN[:, bass.ds(b * T * N + t * N, N)]

        X_LOADS = 4
        x_loaded = [sem(f"x_loaded{i}") for i in range(X_LOADS)]
        par_loaded = sem("par_loaded")
        adj_loaded = [sem(f"adj_loaded{i}") for i in range(2)]
        const_made = sem("const_made")
        prep_pe = sem("prep_pe")
        prep_v = sem("prep_v")
        vchain = sem("vchain")
        vstep = sem("vstep")
        pstep = sem("pstep")
        ln_ready = sem("ln_ready")
        sd_ready = sem("sd_ready")
        sd_root = sem("sd_root")
        names = ["h", "t", "ht"]
        R = {}
        for lay in ("0", "1", "2", "3"):
            for nme in names:
                R[nme + lay] = sem(f"{nme}_ready{lay}")
        z0 = sem("z0_ready"); zm0 = sem("zm0_ready"); zu0 = sem("zu0_ready"); a01_ready = sem("a01_ready")
        agg0 = sem("agg0_ready"); deg0 = sem("deg0"); rdeg0 = sem("rdeg0"); o0 = sem("o0"); xr0 = sem("xr0"); st0 = sem("st0")
        ve1 = sem("ve1_ready"); v1 = sem("v1_ready"); ej1 = sem("ej1_ready"); ei1 = sem("ei1_ready"); zmask1 = sem("zmask1"); zl1 = sem("zl1"); mx1 = sem("mx1")
        p1 = sem("p1_ready"); pt1 = sem("pt1_ready"); ptc1 = sem("ptc1_ready"); o1 = sem("o1_ready")
        r1 = sem("r1"); n1 = sem("n1"); xr1 = sem("xr1"); st1 = sem("st1")
        ht3 = sem("ht3")
        diff_a = sem("diff_a"); abs_a = sem("abs_a"); pair_a = sem("pair_a")
        sq_a = sem("sq_a"); out_a = sem("out_a"); stored_a = [sem(f"stored_a{i}") for i in range(2)]
        back_b = [sem(f"back_b{i}") for i in range(KEPT_SLOTS)]
        consts_b = sem("consts_b")
        diff_b = sem("diff_b"); abs_b = sem("abs_b"); pair_b = sem("pair_b"); relu_b = [sem("kept_relu_b"), sem("made_relu_b")]
        lin_b = sem("lin_b"); direct_b = sem("direct_b"); score_b = sem("score_b")
        s_out = sem("s_out"); skewed = sem("skewed"); zeroed = sem("zeroed"); u_in = sem("u_in")
        full_b = sem("full_b"); mask_b = sem("mask_b"); max_b = sem("max_b"); exp_b = sem("exp_b"); rec_b = sem("rec_b")
        norm_b = sem("norm_b"); tr_b = sem("tr_b"); trc_b = sem("trc_b"); h_b = sem("h_b"); yt_b = sem("yt_b"); ytc_b = sem("ytc_b")
        yg_b = sem("yg_b"); ygs_b = sem("ygs_b"); by_b = sem("by_b")
        bn_y = sem("bn_y"); yl1 = sem("yl1"); yl2 = sem("yl2"); hx = sem("hx"); o2 = sem("o2"); xr2 = sem("xr2"); st2 = sem("st2")
        g3 = sem("g3"); m3 = sem("m3"); mx3 = sem("mx3"); ms3 = sem("ms3"); e3 = sem("e3"); tr3 = sem("tr3"); pt3 = sem("pt3"); hc3 = sem("hc3"); av3 = sem("av3")
        rc3 = sem("rc3"); fin3 = sem("fin3"); stored = [sem(f"stored{i}") for i in range(2)]


        block = ctx.enter_context(nc.Block())

        params = [
            (W01[:, 0:F], w_msg), (W01[:, F:2 * F], w_upd), (WL1[:, :], w_l1),
            (B0[:, :], bias0.rearrange("(a f) -> a f", a=1).broadcast_to([P, F])),
            (BL1[:, :], b_l1.rearrange("(a f) -> a f", a=1).broadcast_to([P, F])),
            (AB[:, :], a_l1.rearrange("d a -> a d").broadcast_to([P, 2 * HD])),
            (W1N[:, :], w1), (WGN[:, :], wg), (WTN[:, :], wt),
            (BTR[:, :], bt.rearrange("(a f) -> a f", a=1)),
            (B2C, b2.rearrange("(a f) -> a f", a=1).broadcast_to([P, 1])),
            (BG, bg.rearrange("(p a) -> p a", a=1)), (GG, gg.rearrange("(p a) -> p a", a=1)),
            (BEG, beg.rearrange("(p a) -> p a", a=1)),
        ]
        for half in range(2):
            rows = slice(half * MID, (half + 1) * MID)
            params += [(PC[rows, 0:1], b1.rearrange("(p a) -> p a", a=1)),
                       (PC[rows, 1:2], g1.rearrange("(p a) -> p a", a=1)),
                       (PC[rows, 2:3], be1.rearrange("(p a) -> p a", a=1)),
                       (PC[rows, 3:4], w2.rearrange("a p -> p a"))]

        @block.sync
        def _(sp):
            per = B // X_LOADS
            for i in range(X_LOADS):
                src = x[i * per:(i + 1) * per].rearrange("b (t p) f -> p (b t) f", p=P)
                dst = XR[:, i * per * N:(i + 1) * per * N].rearrange("p (g f) -> p g f", f=F)
                sp.dma_start(dst, src).then_inc(x_loaded[i], 16)
                if i == 0:
                    for dst, src in params:
                        with nc.allow_non_contiguous_dma(reason="a few parameters"):
                            sp.dma_start(dst, src).then_inc(par_loaded, 16)

            def known(value):
                return value if isinstance(value, int) else sp.snap(value)

            def load_adj(b, s):
                start, used = known(b * (N * N)), known(b - 1)
                wait(sp, a01_ready, used)
                sp.dma_start(AJ[:, s, :].rearrange("p (t j) -> p t j", t=T),
                             bass.AP(adj.tensor, start, [[N, P], [P * N, T], [1, N]])).then_inc(adj_loaded[s], 16)
            for b in range(2):
                load_adj(b, b)
            with sp.Fori(1, B // 2) as pair:
                load_adj(pair * 2, 0)
                load_adj(pair * 2 + 1, 1)

            def keep(b):
                for m in range(KEPT):
                    start, ready = known(b * (KEPT * P * CHUNK)), known(b * KEPT + m + 1)
                    sp.wait_ge(out_a, ready)
                    sp.dma_start(bass.AP(kept, start + m * P * CHUNK, [[CHUNK, P], [1, CHUNK]]),
                                 L[:, m % 2, :]).then_inc(stored_a[m % 2], 16)
            with sp.Fori(0, B) as b:
                keep(b)
            for i in range(2):
                sp.wait_ge(stored_a[i], 16 * B * KEPT // 2)

            sp.wait_ge(zeroed, 1)
            sp.dma_start(skew[:, :, :].rearrange("t p j -> p t j"), U[:, :, :]).then_inc(skewed, 16)
            sp.wait_ge(skewed, 16)

            def back(b, m):
                start, used = known(b * (KEPT * P * CHUNK)), known(b * STEPS + 2 * (m - KEPT_SLOTS) + 1)
                wait(sp, score_b, used)
                sp.dma_start(K[:, m % KEPT_SLOTS, :],
                             bass.AP(kept, start + m * P * CHUNK, [[CHUNK, P], [1, CHUNK]])).then_inc(back_b[m % KEPT_SLOTS], 16)

            def bounce(b):
                sp.wait_ge(s_out, b + 1)
                sp.dma_start(bass.AP(skew, 1, [[N + 1, P], [1, HALF]]), SS[:, 0:HALF]).then_inc(skewed, 16)
                sp.dma_start(bass.AP(skew, P * N + 1, [[N + 1, P], [1, HALF - 1]]), SS[:, HALF + 1:N]).then_inc(skewed, 16)
                sp.wait_ge(skewed, b * 32 + 48)
                sp.dma_start(U[:, :, :], skew[:, :, :].rearrange("t p j -> p t j")).then_inc(u_in, 16)

            def second_pass(b):
                for m in range(KEPT):
                    back(b, m)
                    if m == BOUNCE_AT and has(b - 1):
                        bounce(b - 1)
            second_pass(0)
            with sp.Fori(1, B) as b:
                second_pass(b)
            bounce(B - 1)

            def store(b, s):
                start, ready = known(b * (N * F)), known(b + 1)
                sp.wait_ge(fin3, ready)
                sp.dma_start(bass.AP(out.tensor, start, [[F, P], [P * F, T], [1, F]]),
                             OUT[:, s, :].rearrange("p (t f) -> p t f", t=T)).then_inc(stored[s], 16)
            with sp.Fori(0, B // 2) as pair:
                store(pair * 2, 0)
                store(pair * 2 + 1, 1)
            for s in range(2):
                sp.wait_ge(stored[s], 16 * (B // 2))

        @block.gpsimd
        def _(pool):
            pool.memset(ident[:, :], 0.0).then_inc(const_made, 1)
            pool.memset(fold[:, :], 0.0).then_inc(const_made, 1)
            pool.wait_ge(const_made, 2)
            pool.affine_select(out=ident[:, :], in_=ident[:, :], compare_op=ALU.not_equal, fill=1.0,
                               base=0, pattern=[[-1, P]], channel_multiplier=1).then_inc(const_made, 1)
            for n, off in enumerate((0, MID, -MID)):
                pool.affine_select(out=fold[:, :], in_=fold[:, :], compare_op=ALU.not_equal, fill=1.0,
                                   base=off, pattern=[[-1, P]], channel_multiplier=1).then_inc(const_made, 1)
                pool.wait_ge(const_made, 4 + n)
            pool.memset(ones[:, :], 1.0).then_inc(const_made, 1)

        @block.scalar
        def _(act):
            def root(n):
                act.wait_ge(sd_ready, n)
                act.activation(VA, VA, ACT.Sqrt).then_inc(sd_root, 1)

            def normalised(b, s, free, ready):
                wait(act, *free)
                for t in range(T):
                    ins = act.activation(H[:, s, t, :], xr(b, t), ACT.Relu,
                                         bias=NBIAS[:, bass.ds(b * T + t, 1)], scale=RSTD[:, bass.ds(b * T + t, 1)])
                ins.then_inc(ready, 1)

            root(1)
            act.wait_ge(ln_ready, 1)

            def layer0(n, u):
                if has(n):
                    normalised(n, u, (R["t0"], n - 1), R["h0"])
                if has(n - 1):
                    act.wait_ge(R["t0"], n)
                    wait(act, z0, n - 2)
                    act.activation(HT[:, 1 - u, :], PS[1 - u][:, 0:N], ACT.Copy).then_inc(R["ht0"], 1)
                b, s = n - 2, u
                if has(b):
                    act.wait_ge(z0, b + 1)
                    wait(act, agg0, b - 1)
                    act.activation(ZM[:, s, :, 0:F], PW[s][:, 0:T * F].rearrange("p (t f) -> p t f", t=T),
                                   ACT.Copy).then_inc(zm0, 1)
                    wait(act, xr0, b - 1)
                    act.activation(ZU[:, s, :], PW[s][:, 512:512 + N], ACT.Copy).then_inc(zu0, 1)
            sweep(act, 2, layer0)

            root(2)
            act.wait_ge(ln_ready, 2)

            def layer1(n, u):
                b, s = n - 4, u
                if has(b):
                    for t in range(T):
                        act.wait_ge(mx1, b * T + t + 1)
                        for h in range(HEADS):
                            cols = slice(h * N, (h + 1) * N)
                            ins = act.activation(PR[:, s, t, cols], PR[:, s, t, cols], ACT.Exp,
                                                 bias=mx[:, s, t * HEADS + h:t * HEADS + h + 1])
                        ins.then_inc(p1, 1)

                def transposed_out(t):
                    if has(b):
                        act.wait_ge(pt1, b * T + t + 1)
                        wait(act, o1, b - 1)
                        act.activation(PTA[:, s, t, :], PW[2][:, :], ACT.Copy).then_inc(ptc1, 1)
                both = PW[1][:, 512:512 + T * (F + HEADS)].rearrange("p (t f) -> p t f", t=T)
                if has(n - 3):
                    act.wait_ge(ve1, n - 2)
                    wait(act, o1, n - 4)
                    for t in range(T):
                        ins = act.activation(V[:, 1 - u, t, :, 0:HD],
                                             both[:, t, 0:F].rearrange("p (h d) -> p h d", h=HEADS), ACT.Copy)
                    ins.then_inc(v1, 1)
                transposed_out(0)
                if has(n):
                    normalised(n, u, (R["t1"], n - 1), R["h1"])
                if has(n - 1):
                    act.wait_ge(R["t1"], n)
                    wait(act, ej1, n - 2)
                    wait(act, ve1, n - 2)
                    act.activation(HT[:, 1 - u, :], PW[1][:, 0:N], ACT.Copy).then_inc(R["ht1"], 1)
                if has(n - 2):
                    act.wait_ge(ve1, n - 1)
                    wait(act, zmask1, (n - 3) * T)
                    act.activation(EI[:, u, :, :], both[:, :, F:F + HEADS], ACT.Copy).then_inc(ei1, 1)
                transposed_out(1)
            sweep(act, 4, layer1)

            root(3)
            act.wait_ge(ln_ready, 3)

            def layer2(n, u):
                if has(n):
                    normalised(n, u, (R["t2"], n - 1), R["h2"])
            sweep(act, 0, layer2)

            def first_pass(b):
                for k in range(STEPS):
                    n = b * STEPS + k
                    act.wait_ge(diff_a, n + 1)
                    act.activation(D[:, k % RING, :, :], D[:, k % RING, :, :], ACT.Abs,
                                   accum_out=SD[:, bass.ds(n, 1)]).then_inc(abs_a, 1)
                    if k >= SQ_LAG:
                        squares(b, k - SQ_LAG)
                    elif has(b - 1):
                        squares(b - 1, k - SQ_LAG + STEPS)

            def squares(b, k):
                n = b * STEPS + k
                if is_kept(k):
                    act.wait_ge(out_a, b * KEPT + k // 2 + 1)
                else:
                    act.wait_ge(pair_a, n + 1)
                act.activation(PW[k % PAIR_BANKS], PW[k % PAIR_BANKS], ACT.Square,
                               accum_out=SQ[:, bass.ds(n, 1)]).then_inc(sq_a, 1)
            first_pass(0)
            with act.Fori(1, B) as b:
                first_pass(b)
            for k in range(STEPS - SQ_LAG, STEPS):
                squares(B - 1, k)

            act.wait_ge(sd_ready, 4)
            act.activation(SCALE1, SCALE1, ACT.Sqrt).then_inc(sd_root, 1)
            act.wait_ge(consts_b, 1)

            def relus(b, k):
                if is_kept(k):
                    m = k // 2
                    wait(act, lin_b, b * KEPT + m)
                    act.wait_ge(back_b[m % KEPT_SLOTS], (b * (KEPT // KEPT_SLOTS) + m // KEPT_SLOTS + 1) * 16)
                    source = K[:, m % KEPT_SLOTS, :]
                else:
                    wait(act, score_b, b * STEPS + k - 1)
                    act.wait_ge(pair_b, b * MADE + k // 2 + 1)
                    source = PW[k // 2 % 2]
                act.activation(L[:, k % 2, :], source, ACT.Relu, bias=SHIFT1, scale=SCALE1).then_inc(relu_b[k % 2], 1)

            def second_pass(b):
                for k in range(STEPS):
                    if not is_kept(k):
                        d = D[:, k // 2 % RING, :, :]
                        act.wait_ge(diff_b, b * MADE + k // 2 + 1)
                        act.activation(d, d, ACT.Abs).then_inc(abs_b, 1)
                        if k > 1:
                            relus(b, k - 1)
                            relus(b, k - 2)
                        else:
                            if has(b - 1):
                                relus(b - 1, STEPS - 1)
                            relus(b, 0)
                    act_tail(b - 1, k)

            def act_tail(b, k):
                if k == YG_OUT_AT and has(b - 1):
                    act.wait_ge(yg_b, b)
                    act.activation(YG[:, bass.ds((b - 1) * N, N)], PS[1][:, N:2 * N], ACT.Identity, bias=BG).then_inc(ygs_b, 1)
                if not has(b):
                    return
                if k == S_OUT_AT:
                    act.wait_ge(score_b, (b + 1) * STEPS)
                    wait(act, skewed, b * 32 + 16 if not isinstance(b, int) or b > 0 else 0)
                    act.activation(SS[:, :], PW[2][:, 0:N], ACT.Identity, bias=C0).then_inc(s_out, 1)
                if k == 6:
                    wait(act, yt_b, b)
                    for t in range(T):
                        ins = act.activation(H[:, 0, t, :], xr(b, t), ACT.Relu,
                                             bias=NBIAS[:, bass.ds(b * T + t, 1)], scale=RSTD[:, bass.ds(b * T + t, 1)])
                    ins.then_inc(h_b, 1)
                if k == EXP_AT:
                    act.wait_ge(max_b, b + 1)
                    for t in range(T):
                        ins = act.activation(SM[:, 0, t * N:(t + 1) * N], SM[:, 0, t * N:(t + 1) * N], ACT.Exp,
                                             bias=mx[:, 0, t:t + 1], accum_out=rs[:, 0, t:t + 1])
                    ins.then_inc(exp_b, 1)
            second_pass(0)
            second_pass(1)
            with act.Fori(2, B) as b:
                second_pass(b)
            relus(B - 1, STEPS - 1)
            for b in (B - 1, B):
                for k in range(STEPS):
                    act_tail(b, k)
            act.wait_ge(sd_ready, 5)
            act.activation(SCALEY, SCALEY, ACT.Sqrt).then_inc(sd_root, 1)

            def project(n, u):
                if has(n):
                    wait(act, yl2, n - 1)
                    act.activation(SM3[:, u, 0:N], YG[:, bass.ds(n * N, N)], ACT.Identity, bias=SHIFTY,
                                   scale=SCALEY).then_inc(yl1, 1)
                if has(n - 1):
                    wait(act, o2, n - 2)
                    act.activation(HT[:, 1 - u, :], HT3[:, bass.ds((n - 1) * WRAP, N)], ACT.Copy).then_inc(hx, 1)
            act.wait_ge(bn_y, 1)
            sweep(act, 1, project)

            root(6)
            act.wait_ge(ln_ready, 4)

            def layer3(n, u):
                b, s = n - 4, u
                if has(b):
                    act.wait_ge(ms3, b + 1)
                    for t in range(T):
                        cols = slice(t * N, (t + 1) * N)
                        ins = act.activation(SM3[:, s, cols], SM3[:, s, cols], ACT.Exp, bias=mx[:, s, 2 + t:3 + t],
                                             scale=SCORE_SCALE, accum_out=rs[:, s, t:t + 1])
                    ins.then_inc(e3, 1)
                if has(n):
                    wait(act, hc3, n - 1)
                    normalised(n, u, (R["t3"], n - 1), R["h3"])
                if has(n - 1):
                    act.wait_ge(R["t3"], n)
                    wait(act, g3, n - 2)
                    act.activation(HT[:, 1 - u, :], PS[0][:, 0:N], ACT.Copy).then_inc(R["ht3"], 1)
                if has(b):
                    act.wait_ge(tr3, b + 1)
                    wait(act, av3, b - 1)
                    act.activation(PT3[:, s, :], PS[1][:, :], ACT.Copy).then_inc(pt3, 1)
            sweep(act, 4, layer3)

        @block.tensor
        def _(pe):
            pe.wait_ge(const_made, 7)
            pe.wait_ge(par_loaded, 16 * len(params))
            pe.transpose(PS[0][:, 0:MID], W1N[:, :], ident[0:MID, 0:MID])
            pe.transpose(PS[0][:, P:2 * P], WGN[:, :], ident[:, :])
            pe.transpose(PS[0][:, 2 * P:3 * P], WTN[:, 0:F], ident[:, :])
            pe.transpose(PS[0][:, 3 * P:4 * P], WTN[:, F:2 * F], ident[:, :]).then_inc(prep_pe, 1)
            pe.wait_ge(prep_v, 1)

            def transposes(b, s, bank, h_ready, t_ready):
                pe.wait_ge(h_ready, b + 1)
                for t in range(T):
                    ins = pe.transpose(bank[:, t * P:(t + 1) * P], H[:, s, t, :], ident[:, :])
                ins.then_inc(t_ready, 1)

            def layer0(n, u):
                b, s = n - 3, 1 - u
                if has(b):
                    pe.wait_ge(zm0, b + 1)
                    pe.wait_ge(a01_ready, b + 1)
                    wait(pe, o0, b - 1)
                    for jt in range(T):
                        for it in range(T):
                            ins = pe.matmul(PW[2][:, s * 512 + jt * N:s * 512 + jt * N + F + 1],
                                            A01[:, s, it * N + jt * P:it * N + (jt + 1) * P], ZM[:, s, it, :],
                                            start=it == 0, stop=it == T - 1)
                    ins.then_inc(agg0, 1)
                if has(n - 1):
                    wait(pe, R["ht0"], n - 2)
                    transposes(n - 1, 1 - u, PS[1 - u], R["h0"], R["t0"])
                b, s = n - 2, u
                if has(b):
                    pe.wait_ge(R["ht0"], b + 1)
                    wait(pe, zm0, b - 1)
                    wait(pe, zu0, b - 1)
                    for t in range(T):
                        lhsT = HT[:, s, t * P:(t + 1) * P]
                        update = PW[s][:, 512 + t * F:512 + (t + 1) * F]
                        pe.matmul(PW[s][:, t * F:(t + 1) * F], lhsT, W01[:, 0:F], start=True, stop=True)
                        pe.matmul(update, lhsT, W01[:, F:2 * F], start=True, stop=False)
                        ins = pe.matmul(update, ones[0:1, 0:P], B0[0:1, :], start=False, stop=True)
                    ins.then_inc(z0, 1)
            sweep(pe, 3, layer0)

            def layer1(n, u):
                b, s = n - 5, 1 - u
                if has(b):
                    pe.wait_ge(v1, b + 1)
                    wait(pe, n1, b - 1)
                    for t in range(T):
                        pe.wait_ge(ptc1, b * T + t + 1)
                        for h in range(HEADS):
                            for jt in range(T):
                                at = (t * HEADS + h) * (HD + 1)
                                ins = pe.matmul(PS[s][:, at:at + HD + 1],
                                                PTA[:, s, t, (jt * HEADS + h) * P:(jt * HEADS + h + 1) * P],
                                                V[:, s, jt, h, :], start=jt == 0, stop=jt == T - 1)
                    ins.then_inc(o1, 1)
                if has(n - 1):
                    wait(pe, R["ht1"], n - 1)
                    transposes(n - 1, 1 - u, PW[1], R["h1"], R["t1"])
                if has(n - 2):
                    wait(pe, v1, n - 2)
                    wait(pe, ei1, n - 2)
                    for t in range(T):
                        dst = PW[1][:, 512 + t * (F + HEADS):512 + (t + 1) * (F + HEADS)]
                        pe.matmul(dst, HT[:, u, t * P:(t + 1) * P], WV, start=True, stop=False)
                        ins = pe.matmul(dst, ones[0:1, 0:P], BV, start=False, stop=True)
                    ins.then_inc(ve1, 1)

                def transposed_probabilities(t):
                    b = n - 4
                    if has(b):
                        pe.wait_ge(p1, b * T + t + 1)
                        wait(pe, ptc1, b * T + t)
                        for jt in range(T):
                            for h in range(HEADS):
                                ins = pe.transpose(PW[2][:, (jt * HEADS + h) * P:(jt * HEADS + h + 1) * P],
                                                   PR[:, u, t, h * N + jt * P:h * N + (jt + 1) * P], ident[:, :])
                        ins.then_inc(pt1, 1)
                transposed_probabilities(0)
                transposed_probabilities(1)
                if has(n - 2):
                    pe.wait_ge(R["ht1"], n - 1)
                    wait(pe, zmask1, (n - 2) * T)
                    for h in range(HEADS):
                        ins = pe.matmul(PW[0][:, h * N:(h + 1) * N], WJ[:, h, :], HT[:, u, :], start=True, stop=True)
                    ins.then_inc(ej1, 1)
            sweep(pe, 5, layer1)

            def layer2(n, u):
                if has(n):
                    wait(pe, ht3, n - 1)
                    transposes(n, u, PS[u], R["h2"], R["t2"])
            sweep(pe, 0, layer2)

            def pair_matmuls(d, channels):
                for c in range(2):
                    for half in range(2):
                        ins = pe.matmul(channels[half * MID:(half + 1) * MID, c * 512:(c + 1) * 512], W1T[:, 0:MID],
                                        d[:, half, c * 512:(c + 1) * 512], start=True, stop=True)
                return ins

            def first_pass(b):
                for k in range(STEPS):
                    n = b * STEPS + k
                    pe.wait_ge(abs_a, n + 1)
                    wait(pe, sq_a, n - PAIR_BANKS + 1)
                    pair_matmuls(D[:, k % RING, :, :], PW[k % PAIR_BANKS]).then_inc(pair_a, 1)
            first_pass(0)
            with pe.Fori(1, B) as b:
                first_pass(b)

            pe.wait_ge(vstep, 1)
            pe.matmul(PS[0][:, 0:1], W1T[:, :], small[:, 0:1], start=True, stop=True)
            pe.matmul(PS[0][:, 1:2], fold[:, :], small[:, 2:3], start=True, stop=True).then_inc(pstep, 1)
            pe.wait_ge(vstep, 2)
            pe.matmul(PS[0][:, 0:1], W1N[:, :], small[0:MID, 16:17], start=True, stop=True)
            pe.matmul(PS[0][:, 2:4], ones[0:MID, :], small[0:MID, 17:19], start=True, stop=True).then_inc(pstep, 1)
            pe.wait_ge(consts_b, 1)

            def score_matmuls(b, k):
                if is_kept(k):
                    pe.wait_ge(lin_b, b * KEPT + k // 2 + 1)
                else:
                    pe.wait_ge(relu_b[1], b * MADE + k // 2 + 1)
                at = ROWS - 1 - 2 * k
                rectified = K[:, k // 2 % KEPT_SLOTS, :] if is_kept(k) else L[:, 1, :]
                for g in range(GROUPS):
                    ins = pe.matmul(PW[2][g * ROWS:(g + 1) * ROWS, 0:N], W2P[:, at:at + ROWS],
                                    rectified[:, g * N:(g + 1) * N], start=False, stop=k == STEPS - 1)
                ins.then_inc(score_b, 1)

            def linear_matmuls(k):
                at = ROWS - 1 - 2 * k
                for half in range(2):
                    for g in range(GROUPS):
                        ins = pe.matmul(PW[2][g * ROWS:(g + 1) * ROWS, 0:N], VP[:, at - half:at - half + ROWS],
                                        D[:, k // 2 % RING, half, g * N:(g + 1) * N], start=k == 1 and half == 0,
                                        stop=False)
                ins.then_inc(direct_b, 1)

            def second_pass(b):
                for k in range(STEPS):
                    if not is_kept(k):
                        n = b * MADE + k // 2
                        pe.wait_ge(abs_b, n + 1)
                        wait(pe, relu_b[1], n - 1)
                        pair_matmuls(D[:, k // 2 % RING, :, :], PW[k // 2 % 2]).then_inc(pair_b, 1)
                        if k == 1:
                            if has(b - 1):
                                score_matmuls(b - 1, STEPS - 1)
                            wait(pe, s_out, b)
                            linear_matmuls(1)
                            score_matmuls(b, 0)
                        else:
                            linear_matmuls(k)
                            score_matmuls(b, k - 2)
                            score_matmuls(b, k - 1)
                    pe_tail(b - 1, k)

            def pe_tail(b, k):
                if k == YG_AT and has(b - 1):
                    pe.wait_ge(ytc_b, b)
                    pe.matmul(PS[1][:, N:2 * N], WGT[:, :], YT[:, :], start=True, stop=True).then_inc(yg_b, 1)
                if not has(b):
                    return
                if k == FULL_AT:
                    pe.wait_ge(u_in, (b + 1) * 16)
                    wait(pe, mask_b, b)
                    blocks = [(U[:, 0, 0:P], U[:, 0, 0:P], True), (U[:, 0, P:N], U[:, 1, P:N], False),
                              (U[:, 1, P:N], U[:, 0, P:N], False), (U[:, 1, 0:P], U[:, 1, 0:P], True)]
                    for i, (own, other, diagonal) in enumerate(blocks):
                        dst = PS[0][:, i * P:(i + 1) * P]
                        pe.matmul(dst, ident[:, :], own, start=True, stop=False)
                        ins = pe.matmul(dst, other, ident[:, :], start=False, stop=not diagonal)
                        if diagonal:
                            ins = pe.matmul(dst, ident[:, :], eye0[:, :], start=False, stop=True)
                    ins.then_inc(full_b, 1)
                if k == TR_AT:
                    pe.wait_ge(norm_b, b + 1)
                    wait(pe, ygs_b, b)
                    for jt in range(T):
                        for it in range(T):
                            ins = pe.transpose(PS[1][:, jt * N + it * P:jt * N + (it + 1) * P],
                                               SM[:, 0, it * N + jt * P:it * N + (jt + 1) * P], ident[:, :])
                    ins.then_inc(tr_b, 1)
                if k == YT_AT:
                    pe.wait_ge(trc_b, b + 1)
                    pe.wait_ge(h_b, b + 1)
                    for jt in range(T):
                        ins = pe.matmul(PS[1][:, 0:N], H[:, 0, jt, :], PT[:, 0, jt * N:(jt + 1) * N],
                                        start=jt == 0, stop=jt == T - 1)
                    ins.then_inc(yt_b, 1)
            second_pass(0)
            second_pass(1)
            with pe.Fori(2, B) as b:
                second_pass(b)
            score_matmuls(B - 1, STEPS - 1)
            for b in (B - 1, B):
                for k in range(STEPS):
                    pe_tail(b, k)

            def project(n, u):
                b, s = n - 2, u
                if has(b):
                    pe.wait_ge(yl2, b + 1)
                    pe.wait_ge(hx, b + 1)
                    wait(pe, xr2, b - 1)
                    for t in range(T):
                        dst = PS[s][:, t * F:(t + 1) * F]
                        cols = slice(t * P, (t + 1) * P)
                        pe.matmul(dst, HT[:, s, cols], WTT[:, 0, :], start=True, stop=False)
                        pe.matmul(dst, PT3[:, s, cols], WTT[:, 1, :], start=False, stop=False)
                        ins = pe.matmul(dst, ones[0:1, 0:P], BTR[:, :], start=False, stop=True)
                    ins.then_inc(o2, 1)
            sweep(pe, 2, project)

            def layer3(n, u):
                b, s = n - 5, 1 - u
                if has(b):
                    pe.wait_ge(pt3, b + 1)
                    wait(pe, fin3, b - 1)
                    for it in range(T):
                        for jt in range(T):
                            ins = pe.matmul(PW[2][:, s * 512 + it * F:s * 512 + (it + 1) * F],
                                            PT3[:, s, jt * N + it * P:jt * N + (it + 1) * P],
                                            YG[:, bass.ds(b * N + jt * F, F)], start=jt == 0, stop=jt == T - 1)
                    ins.then_inc(av3, 1)
                if has(n - 1):
                    wait(pe, R["ht3"], n - 1)
                    transposes(n - 1, 1 - u, PS[0], R["h3"], R["t3"])
                b, s = n - 2, u
                if has(b):
                    pe.wait_ge(R["ht3"], b + 1)
                    wait(pe, m3, b - 1)
                    for t in range(T):
                        ins = pe.matmul(PW[s][:, t * N:(t + 1) * N], HT[:, s, t * P:(t + 1) * P], HT[:, s, :],
                                        start=True, stop=True)
                    ins.then_inc(g3, 1)
                b, s = n - 4, u
                if has(b):
                    pe.wait_ge(e3, b + 1)
                    wait(pe, pt3, b)
                    for jt in range(T):
                        for it in range(T):
                            ins = pe.transpose(PS[1][:, jt * N + it * P:jt * N + (it + 1) * P],
                                               SM3[:, s, it * N + jt * P:it * N + (jt + 1) * P], ident[:, :])
                    ins.then_inc(tr3, 1)
            sweep(pe, 5, layer3)

        @block.vector
        def _(dve):
            done = [0]

            def chain(ins):
                done[0] += 1
                ins.then_inc(own, 1)
                dve.wait_ge(own, done[0])

            own = vchain

            def ln_stats(b):
                for t in range(T):
                    ins = dve.bn_stats(ST[:, bass.ds((b * T + t) * 6, 6)], xr(b, t))
                return ins

            def ln_finish(n_root, n_ln):
                s = ST[:, :].rearrange("p (g k) -> p g k", k=6)
                chain(dve.tensor_tensor(MS[:, :], s[:, :, 1], s[:, :, 4], ALU.add))
                chain(dve.tensor_tensor(VB[:, :], s[:, :, 1], s[:, :, 4], ALU.subtract))
                chain(dve.tensor_tensor(VA, s[:, :, 2], s[:, :, 5], ALU.add))
                chain(dve.tensor_tensor(VB[:, :], VB[:, :], VB[:, :], ALU.mult))
                chain(dve.tensor_scalar(VA, VA, 1.0 / F, EPS, ALU.mult, ALU.add))
                dve.scalar_tensor_tensor(VA, VB[:, :], 0.25, VA, ALU.mult, ALU.add).then_inc(sd_ready, 1)
                dve.wait_ge(sd_root, n_root)
                chain(dve.reciprocal(RSTD[:, :], VA))
                dve.scalar_tensor_tensor(NBIAS[:, :], MS[:, :], -0.5, RSTD[:, :], ALU.mult, ALU.mult).then_inc(ln_ready, 1)

            for i in range(X_LOADS):
                dve.wait_ge(x_loaded[i], 16)
                with dve.Fori(0, B // X_LOADS // 4) as four:
                    for g in range(4):
                        ln_stats(four * 4 + (i * (B // X_LOADS) + g)).then_inc(st0, 1)
            dve.wait_ge(st0, B)
            ln_finish(1, 1)

            chain(dve.memset(ZM[:, :, :, F:F + 1], 1.0))
            dve.wait_ge(par_loaded, 16 * len(params))
            ab = AB[:, :].rearrange("p (s d) -> p s d", s=2)
            for side in range(2):
                for h in range(HEADS):
                    chain(dve.tensor_tensor(WM[:, side * HEADS + h, :], WL1[:, h * HD:(h + 1) * HD], ab[:, side, :], ALU.mult))
            chain(dve.tensor_reduce(WA[:, :], WM, AX_X, ALU.add))
            for side in range(2):
                for h in range(HEADS):
                    chain(dve.tensor_tensor(WM[:, side * HEADS + h, :], BL1[:, h * HD:(h + 1) * HD], ab[:, side, :], ALU.mult))
            chain(dve.tensor_reduce(CE[:, :], WM, AX_X, ALU.add))
            chain(dve.tensor_tensor(BV[:, F:F + HEADS], CE[0:1, 0:HEADS], CE[0:1, HEADS:2 * HEADS], ALU.add))
            dve.tensor_copy(BV[:, 0:F], BL1[0:1, :])
            dve.tensor_copy(WV[:, F:F + HEADS], WA[:, 0:HEADS])
            dve.tensor_copy(WJ, WA[:, HEADS:2 * HEADS].rearrange("p (h a) -> p h a", a=1).broadcast_to([P, HEADS, P]))
            dve.wait_ge(prep_pe, 1)
            for half in range(2):
                dve.tensor_copy(W1T[:, half * MID:(half + 1) * MID], PS[0][:, 0:MID])
            dve.tensor_copy(WGT[:, :], PS[0][:, P:2 * P])
            dve.tensor_copy(WTT[:, :, :].rearrange("p a f -> p (a f)"), PS[0][:, 2 * P:4 * P]).then_inc(prep_v, 1)

            def layer0(n, u):
                b, s = n - 4, u
                acc = PW[2][:, s * 512:s * 512 + T * N].rearrange("p (t f) -> p t f", t=T)
                if has(b):
                    dve.wait_ge(agg0, b + 1)
                    dve.tensor_scalar(rs[:, s, 0:T], acc[:, :, F], 1.0, None, ALU.max).then_inc(deg0, 1)
                if has(n - 2):
                    dve.wait_ge(adj_loaded[u], (n // 2) * 16 if isinstance(n, int) else (n - u) * 8)
                    dve.tensor_scalar(mn(n - 2), AJ[:, u, :], 0.0, NEG, ALU.is_le, ALU.mult)
                if has(b):
                    dve.wait_ge(deg0, b + 1)
                    dve.reciprocal(rs[:, s, 2:2 + T], rs[:, s, 0:T]).then_inc(rdeg0, 1)
                if has(n - 2):
                    wait(dve, agg0, n - 3)
                    dve.tensor_scalar(A01[:, u, :], AJ[:, u, :], 0.0, None, ALU.not_equal).then_inc(a01_ready, 1)
                if has(b):
                    dve.wait_ge(rdeg0, b + 1)
                    dve.wait_ge(zu0, b + 1)
                    for t in range(T):
                        cols = slice(t * F, (t + 1) * F)
                        ins = dve.scalar_tensor_tensor(ZU[:, s, cols], acc[:, t, 0:F], rs[:, s, 2 + t:3 + t],
                                                       ZU[:, s, cols], ALU.mult, ALU.add)
                    ins.then_inc(o0, 1)
                if has(n - 5):
                    dve.wait_ge(xr0, n - 4)
                    ln_stats(n - 5).then_inc(st0, 1)
                if has(b):
                    dve.wait_ge(o0, b + 1)
                    dve.scalar_tensor_tensor(xr(b), ZU[:, s, :], 0.0, xr(b), ALU.max, ALU.add).then_inc(xr0, 1)
            sweep(dve, 5, layer0)
            dve.wait_ge(st0, 2 * B)
            ln_finish(2, 2)

            chain(dve.memset(V[:, :, :, :, HD:HD + 1], 1.0))

            def layer1(n, u):
                b, s = n - 3, 1 - u
                if has(b):
                    dve.wait_ge(ej1, b + 1)
                    dve.wait_ge(ei1, b + 1)
                    wait(dve, pt1, (b - 1) * T)
                    for t in range(T):
                        for h in range(HEADS):
                            cols = slice(h * N, (h + 1) * N)
                            ins = dve.scalar_tensor_tensor(PR[:, s, t, cols], PW[0][:, cols], EI[:, s, t, h:h + 1],
                                                           mn(b, t), ALU.add, ALU.add)
                        ins.then_inc(zmask1, 1)
                    for t in range(T):
                        dve.wait_ge(zmask1, b * T + t + 1)
                        dve.scalar_tensor_tensor(PR[:, s, t, :], PR[:, s, t, :], 0.2, PR[:, s, t, :], ALU.mult,
                                                 ALU.max).then_inc(zl1, 1)
                    for t in range(T):
                        dve.wait_ge(zl1, b * T + t + 1)
                        dve.tensor_reduce(mx[:, s, t * HEADS:(t + 1) * HEADS],
                                          PR[:, s, t, :].rearrange("p (h j) -> p h j", h=HEADS), AX_X, ALU.max,
                                          negate=True).then_inc(mx1, 1)
                b, s = n - 5, 1 - u
                if has(b):
                    dve.wait_ge(o1, b + 1)
                    o = PS[s][:, 0:T * HEADS * (HD + 1)].rearrange("p (h d) -> p h d", d=HD + 1)
                    dve.reciprocal(rs[:, s, :], o[:, :, HD]).then_inc(r1, 1)
                    dve.wait_ge(r1, b + 1)
                    per_head = rs[:, s, :].rearrange("p (h a) -> p h a", a=1).broadcast_to([P, T * HEADS, HD])
                    dve.tensor_tensor(TMP.rearrange("p (h d) -> p h d", d=HD), o[:, :, 0:HD], per_head,
                                      ALU.mult).then_inc(n1, 1)
                    dve.wait_ge(n1, b + 1)
                    dve.tensor_tensor(xr(b), xr(b), TMP, ALU.add).then_inc(xr1, 1)
                    dve.wait_ge(xr1, b + 1)
                    ln_stats(b).then_inc(st1, 1)
            sweep(dve, 5, layer1)
            dve.wait_ge(st1, B)
            ln_finish(3, 3)

            def layer2(n, u):
                if has(n):
                    dve.wait_ge(R["t2"], n + 1)
                    dve.tensor_copy(HT3[:, bass.ds(n * WRAP, N)], PS[u][:, 0:N])
                    dve.tensor_copy(HT3[:, bass.ds(n * WRAP + N, HALF)], PS[u][:, 0:HALF]).then_inc(ht3, 1)
            sweep(dve, 0, layer2)
            dve.wait_ge(ht3, B)

            def differences(b, k, slot, halves=(0, 1)):
                for half in halves:
                    at = b * WRAP + 2 * k + half
                    ahead = bass.AP(HT3, at + 1, [[B * WRAP, P], [ROWS, GROUPS], [P - 1, T], [1, HALF]])
                    here = bass.AP(HT3, at, [[B * WRAP, P], [ROWS, GROUPS], [P, T], [0, HALF]])
                    ins = dve.tensor_tensor(D[:, slot, half, :].rearrange("p (g t d) -> p g t d", g=GROUPS, t=T),
                                            ahead, here, ALU.subtract)
                return ins

            def take_out(b, k):
                if not is_kept(k):
                    return
                m = k // 2
                dve.wait_ge(pair_a, b * STEPS + k + 1)
                wait(dve, stored_a[m % 2], (b * (KEPT // 2) + m // 2) * 16)
                dve.tensor_copy(L[:, m % 2, :], PW[k % PAIR_BANKS]).then_inc(out_a, 1)

            def first_pass(b):
                for k in range(STEPS):
                    wait(dve, pair_a, b * STEPS + k - RING + 1)
                    differences(b, k, k % RING).then_inc(diff_a, 1)
                    if k >= KEEP_LAG:
                        take_out(b, k - KEEP_LAG)
                    elif has(b - 1):
                        take_out(b - 1, k - KEEP_LAG + STEPS)
            first_pass(0)
            with dve.Fori(1, B) as b:
                first_pass(b)
            for k in range(STEPS - KEEP_LAG, STEPS):
                take_out(B - 1, k)

            dve.wait_ge(abs_a, B * STEPS)
            dve.wait_ge(sq_a, B * STEPS)
            sm = small
            chain(dve.tensor_reduce(sm[:, 0:1], SD, AX_X, ALU.add))
            dve.tensor_reduce(sm[:, 2:3], SQ, AX_X, ALU.add).then_inc(vstep, 1)
            dve.wait_ge(pstep, 1)
            chain(dve.tensor_scalar(sm[:, 8:10], PS[0][:, 0:2], 2.0 / PAIRS, None, ALU.mult))
            chain(dve.tensor_tensor(sm[:, 10:11], sm[:, 8:9], sm[:, 8:9], ALU.mult))
            chain(dve.tensor_tensor(sm[:, 11:12], sm[:, 9:10], sm[:, 10:11], ALU.subtract))
            dve.tensor_scalar(SCALE1, sm[:, 11:12], EPS, None, ALU.add).then_inc(sd_ready, 1)
            dve.wait_ge(sd_root, 4)
            chain(dve.reciprocal(sm[:, 12:13], SCALE1))
            chain(dve.tensor_tensor(SCALE1, sm[:, 12:13], G1, ALU.mult))
            chain(dve.tensor_scalar(SLIN, SCALE1, 0.01 / 0.99, None, ALU.mult))
            chain(dve.tensor_tensor(sm[:, 13:14], sm[:, 8:9], B1, ALU.add))
            chain(dve.tensor_tensor(sm[:, 13:14], B1, sm[:, 13:14], ALU.subtract))
            chain(dve.scalar_tensor_tensor(SHIFT1, sm[:, 13:14], SCALE1, BE1, ALU.mult, ALU.add))
            chain(dve.tensor_scalar(sm[:, 14:15], W2C, 0.01, None, ALU.mult))
            chain(dve.tensor_scalar(sm[:, 15:16], W2C, 0.99, None, ALU.mult))
            chain(dve.tensor_tensor(sm[:, 16:17], sm[:, 14:15], SCALE1, ALU.mult))
            chain(dve.tensor_tensor(sm[:, 17:18], sm[:, 14:15], SHIFT1, ALU.mult))
            dve.scalar_tensor_tensor(sm[:, 18:19], SHIFT1, 0.0, sm[:, 15:16], ALU.max, ALU.mult).then_inc(vstep, 1)
            dve.memset(W2P[:, :], 0.0)
            chain(dve.memset(VP[:, :], 0.0))
            dve.memset(U[:, :, :], 0.0).then_inc(zeroed, 1)
            for half in range(2):
                rows = slice(half * MID, (half + 1) * MID)
                chain(dve.tensor_copy(W2P[rows, ROWS - 1 + half:ROWS + half], sm[rows, 15:16]))
            dve.wait_ge(pstep, 2)
            chain(dve.tensor_copy(VP[:, ROWS - 1:ROWS], PS[0][:, 0:1]))
            chain(dve.tensor_tensor(C0, PS[0][:, 2:3], B2C, ALU.add))
            chain(dve.tensor_tensor(SC0, PS[0][:, 3:4], C0, ALU.add))
            dve.tensor_scalar(eye0[:, :], ident[:, :], SC0, None, ALU.mult).then_inc(consts_b, 1)
            dve.wait_ge(zeroed, 1)

            def second_pass(b):
                for k in range(STEPS):
                    if not is_kept(k):
                        m = k // 2
                        wait(dve, direct_b, b * MADE + m - RING + 1)
                        differences(b, k, m % RING, [0])
                        if k > LINEAR_LAG:
                            linear(b, k - 1 - LINEAR_LAG)
                        elif has(b - 1):
                            linear(b - 1, k - 1 - LINEAR_LAG + STEPS)
                        differences(b, k, m % RING, [1]).then_inc(diff_b, 1)
                    dve_tail(b - 1, k)

            def linear(b, k):
                dve.wait_ge(relu_b[0], b * KEPT + k // 2 + 1)
                both = K[:, k // 2 % KEPT_SLOTS, :]
                dve.scalar_tensor_tensor(both, both, SLIN, L[:, 0, :], ALU.mult, ALU.add).then_inc(lin_b, 1)

            def dve_tail(b, k):
                if k == TRC_AT and has(b - 1):
                    dve.wait_ge(tr_b, b)
                    wait(dve, yt_b, b - 1)
                    dve.tensor_copy(PT[:, 0, :], PS[1][:, :]).then_inc(trc_b, 1)
                if k == YTC_AT and has(b - 1):
                    dve.wait_ge(yt_b, b)
                    wait(dve, yg_b, b - 1)
                    dve.tensor_copy(YT[:, :], PS[1][:, 0:N]).then_inc(ytc_b, 1)
                if k == BY_AT and has(b - 1):
                    dve.wait_ge(ygs_b, b)
                    dve.bn_stats(BY[:, bass.ds((b - 1) * 6, 6)], YG[:, bass.ds((b - 1) * N, N)]).then_inc(by_b, 1)
                if not has(b):
                    return
                if k == MASK_AT:
                    dve.wait_ge(full_b, b + 1)
                    wait(dve, tr_b, b)
                    dve.tensor_tensor(SM[:, 0, :], PS[0][:, :], mn(b), ALU.add).then_inc(mask_b, 1)
                    dve.wait_ge(mask_b, b + 1)
                    dve.tensor_reduce(mx[:, 0, 0:T], SM[:, 0, :].rearrange("p (t j) -> p t j", t=T), AX_X, ALU.max,
                                      negate=True).then_inc(max_b, 1)
                if k == NORM_AT:
                    dve.wait_ge(exp_b, b + 1)
                    dve.reciprocal(rs[:, 0, 2:2 + T], rs[:, 0, 0:T]).then_inc(rec_b, 1)
                    dve.wait_ge(rec_b, b + 1)
                    for t in range(T):
                        cols = slice(t * N, (t + 1) * N)
                        ins = dve.tensor_scalar(SM[:, 0, cols], SM[:, 0, cols], rs[:, 0, 2 + t:3 + t], None, ALU.mult)
                    ins.then_inc(norm_b, 1)
            second_pass(0)
            second_pass(1)
            with dve.Fori(2, B) as b:
                second_pass(b)
            for k in range(STEPS - LINEAR_LAG, STEPS, 2):
                linear(B - 1, k)
            for b in (B - 1, B):
                for k in range(STEPS):
                    dve_tail(b, k)
            dve.wait_ge(by_b, B)
            chain(dve.bn_aggr(MV[:, 0:2], BY[:, :].rearrange("p (g k) -> p g k", k=6)))
            dve.tensor_scalar(SCALEY, MV[:, 1:2], EPS, None, ALU.add).then_inc(sd_ready, 1)
            dve.wait_ge(sd_root, 5)
            chain(dve.reciprocal(MV[:, 2:3], SCALEY))
            chain(dve.tensor_tensor(SCALEY, MV[:, 2:3], GG, ALU.mult))
            chain(dve.tensor_tensor(MV[:, 3:4], MV[:, 0:1], SCALEY, ALU.mult))
            dve.tensor_tensor(SHIFTY, BEG, MV[:, 3:4], ALU.subtract).then_inc(bn_y, 1)

            def project(n, u):
                b, s = n - 3, 1 - u
                if has(b):
                    dve.wait_ge(o2, b + 1)
                    dve.tensor_tensor(xr(b), xr(b), PS[s][:, 0:N], ALU.add).then_inc(xr2, 1)
                if has(n - 1):
                    dve.wait_ge(yl1, n)
                    wait(dve, o2, n - 2)
                    dve.scalar_tensor_tensor(PT3[:, 1 - u, 0:N], SM3[:, 1 - u, 0:N], 0.01, SM3[:, 1 - u, 0:N],
                                             ALU.mult, ALU.max).then_inc(yl2, 1)
                if has(b):
                    dve.wait_ge(xr2, b + 1)
                    ln_stats(b).then_inc(st2, 1)
            sweep(dve, 3, project)
            dve.wait_ge(st2, B)
            ln_finish(6, 4)

            def layer3(n, u):
                b, s = n - 3, 1 - u
                if has(b):
                    dve.wait_ge(g3, b + 1)
                    wait(dve, tr3, b - 1)
                    dve.tensor_tensor(SM3[:, s, :], PW[s][:, 0:T * N], mn(b), ALU.add).then_inc(m3, 1)
                if has(n - 1):
                    dve.wait_ge(R["h3"], n)
                    dve.tensor_copy(YG[:, bass.ds((n - 1) * N, N)],
                                    H[:, 1 - u, :, :].rearrange("p t f -> p (t f)")).then_inc(hc3, 1)
                if has(b):
                    dve.wait_ge(m3, b + 1)
                    dve.tensor_reduce(mx[:, s, 0:T], SM3[:, s, :].rearrange("p (t j) -> p t j", t=T), AX_X, ALU.max,
                                      negate=True).then_inc(mx3, 1)
                b, s = n - 5, 1 - u
                if has(b):
                    dve.wait_ge(av3, b + 1)
                    dve.reciprocal(rs[:, s, 2:2 + T], rs[:, s, 0:T]).then_inc(rc3, 1)
                b, s = n - 3, 1 - u
                if has(b):
                    dve.wait_ge(mx3, b + 1)
                    dve.tensor_scalar(mx[:, s, 2:2 + T], mx[:, s, 0:T], SCORE_SCALE, None, ALU.mult).then_inc(ms3, 1)
                b, s = n - 5, 1 - u
                if has(b):
                    dve.wait_ge(rc3, b + 1)
                    if not isinstance(b, int) or b >= 2:
                        dve.wait_ge(stored[s], (b // 2) * 16 if isinstance(b, int) else (b - s) * 8)
                    for t in range(T):
                        ins = dve.scalar_tensor_tensor(OUT[:, s, t * F:(t + 1) * F],
                                                       PW[2][:, s * 512 + t * F:s * 512 + (t + 1) * F],
                                                       rs[:, s, 2 + t:3 + t], xr(b, t), ALU.mult, ALU.add)
                    ins.then_inc(fin3, 1)
            sweep(dve, 5, layer3)


_INS = ['x', 'adj', 'L0_gnn_W_msg', 'L0_gnn_W_upd', 'L0_gnn_bias', 'L1_gnn_W', 'L1_gnn_b', 'L1_gnn_a',
        'L2_gnn_W1', 'L2_gnn_b1', 'L2_gnn_g1', 'L2_gnn_be1', 'L2_gnn_W2', 'L2_gnn_b2', 'L2_gnn_Wg', 'L2_gnn_bg',
        'L2_gnn_gg', 'L2_gnn_beg', 'L2_gnn_Wt', 'L2_gnn_bt']


def kernel(**inputs):
    import numpy as _np
    import concourse.bacc as _bacc
    from concourse import mybir as _mybir
    from concourse.bass_utils import run_bass_kernel_spmd as _run

    nc = _bacc.Bacc("TRN2", target_bir_lowering=False, num_devices=1)
    arrays, args = {}, []
    for name in _INS:
        a = _np.ascontiguousarray(inputs[name])
        arrays[f"in_{name}_dram"] = a
        args.append(nc.dram_tensor(f"in_{name}_dram", a.shape, _mybir.dt.from_np(a.dtype), kind="ExternalInput").ap())
    args.append(nc.dram_tensor("out_dram", (B, N, F), _mybir.dt.float32, kind="ExternalOutput").ap())
    build(nc, *args)
    r = _run(nc, [arrays], core_ids=[0])
    return r.results[0]["out_dram"]
```
